# Optimizing a Trainium2 kernel written in Bass

```python
import numpy as np
import jax
import jax.numpy as jnp

def _softmax(x, axis=-1):
    return jax.nn.softmax(x, axis=axis)

def _gelu(x):
    return jax.nn.gelu(x, approximate=True)

def _silu(x):
    return jax.nn.silu(x)

def _sigmoid(x):
    return jax.nn.sigmoid(x)

def _layernorm(x, axis=-1, eps=1e-05):
    m = jnp.mean(x, axis=axis, keepdims=True)
    v = jnp.var(x, axis=axis, keepdims=True)
    return (x - m) / jnp.sqrt(v + eps)

def _scatter_add(tgt, idx, src, axis=0):
    return tgt.at[idx].add(src)

def _segment_sum(src, seg, n):
    return jax.ops.segment_sum(src, seg, n)
kernel_name = 'mk_decoder_preln_d1_seqx_r4_aee467'

def setup_inputs(seed: int=0):
    np.random.seed(seed)
    _w = jnp.asarray

    def _rec_inputs():
        import jax
        import jax.numpy as jnp
        _rk = jax.random.key(seed)
        x = -0.0003929 + 0.9999 * jax.random.normal(jax.random.fold_in(_rk, 1), (16, 256, 256), jnp.float32)
        _lenS = 256 - jax.random.randint(jax.random.fold_in(_rk, 7), (16,), 0, max(1, 256 // 4) + 1, jnp.int32)
        _lenS2 = 256 - jax.random.randint(jax.random.fold_in(_rk, 8), (16,), 0, max(1, 256 // 4) + 1, jnp.int32)
        _ctx_1024P = jax.random.normal(jax.random.fold_in(_rk, 11), (16, 16, 256), jnp.float32)
        _ctx_1024c = jax.random.dirichlet(jax.random.fold_in(_rk, 511), 0.3 * jnp.ones((16,), jnp.float32), (16, 256))
        _ctx_1024t = jnp.einsum('bsk,bkd->bsd', _ctx_1024c, _ctx_1024P)
        _ctx_1024t = _ctx_1024t * jax.lax.rsqrt(jnp.mean(jnp.square(_ctx_1024t)) + 1e-12) * 0.953939
        ctx_1024 = 2.81802e-05 + 1.00001 * (_ctx_1024t + 0.3 * jax.random.normal(jax.random.fold_in(_rk, 611), (16, 256, 256), jnp.float32))
        return (x, ctx_1024)
    x, ctx_1024 = _rec_inputs()

    def _L0_attn_setup():
        import jax, jax.numpy as jnp
        import numpy as np
        N_HEAD = 16
        CHUNK = 128

        def _phi(x):
            return jax.nn.elu(x) + 1.0

        def _causal_linear_attn(qp, kp, v):
            B, H, T, D = qp.shape
            NC = T // CHUNK

            def to_chunks(a):
                return a.reshape(B, H, NC, CHUNK, D).transpose(2, 0, 1, 3, 4)
            qc, kc, vc = (to_chunks(qp), to_chunks(kp), to_chunks(v))
            mask = jnp.tril(jnp.ones((CHUNK, CHUNK), dtype=bool))

            def step(carry, blk):
                S, z = carry
                q_c, k_c, v_c = blk
                scores = jnp.einsum('bhcd,bhkd->bhck', q_c, k_c)
                scores = jnp.where(mask, scores, 0.0)
                num = jnp.einsum('bhck,bhke->bhce', scores, v_c) + jnp.einsum('bhcd,bhde->bhce', q_c, S)
                den = scores.sum(-1) + jnp.einsum('bhcd,bhd->bhc', q_c, z)
                S = S + jnp.einsum('bhkd,bhke->bhde', k_c, v_c)
                z = z + k_c.sum(axis=2)
                return ((S, z), (num, den))
            S0 = jnp.zeros((B, H, D, D), dtype=qp.dtype)
            z0 = jnp.zeros((B, H, D), dtype=qp.dtype)
            _, (num, den) = jax.lax.scan(step, (S0, z0), (qc, kc, vc))
            y = num / (den[..., None] + 1e-06)
            y = y.transpose(1, 2, 0, 3, 4).reshape(B, H, T, D)
            return y
        key = jax.random.key(seed)
        k1, k2, k3 = jax.random.split(key, 3)
        B, T, E = (4, 512, 256)
        x = jax.random.normal(k1, (B, T, E), dtype=jnp.float32)
        w_attn = jax.random.normal(k2, (3 * E, E), dtype=jnp.float32) * 0.02
        w_proj = jax.random.normal(k3, (E, E), dtype=jnp.float32) * 0.02
        return {'x': x, 'w_attn': w_attn, 'w_proj': w_proj}
    _L0_attn_all = _L0_attn_setup()
    _L0_attn_in = {k: v for k, v in _L0_attn_all.items() if k in ('w_attn', 'w_proj')}
    del _L0_attn_all

    def _L0_xattn_setup():
        import jax, jax.numpy as jnp
        import numpy as np
        EPS = 1e-08
        LN_EPS = 1e-05

        def _layernorm(x, g, b):
            mu = jnp.mean(x, axis=-1, keepdims=True)
            var = jnp.var(x, axis=-1, keepdims=True)
            return (x - mu) * jax.lax.rsqrt(var + LN_EPS) * g + b

        def _prob(x):
            x = jnp.tanh(x) * 0.499 + 0.5
            return jnp.clip(x / (jnp.sum(x, axis=-1, keepdims=True) + EPS), EPS)
        key = jax.random.key(seed)
        ks = jax.random.split(key, 8)
        B, N, D = (8, 512, 256)
        H = 4 * D
        s = 0.02
        return {'q': jax.random.normal(ks[0], (B, N, D), jnp.float32), 'k': jax.random.normal(ks[1], (B, N, D), jnp.float32), 'v': jax.random.normal(ks[2], (B, N, D), jnp.float32), 'W_diff': jax.random.normal(ks[3], (D, D), jnp.float32) * s, 'b_diff': jnp.zeros((D,), jnp.float32), 'ln_g': jnp.ones((D,), jnp.float32), 'ln_b': jnp.zeros((D,), jnp.float32), 'W1': jax.random.normal(ks[4], (H, D), jnp.float32) * s, 'b1': jnp.zeros((H,), jnp.float32), 'W2': jax.random.normal(ks[5], (D, H), jnp.float32) * s, 'b2': jnp.zeros((D,), jnp.float32)}
    _L0_xattn_all = _L0_xattn_setup()
    _L0_xattn_in = {k: v for k, v in _L0_xattn_all.items() if k in ('W_diff', 'b_diff', 'ln_g', 'ln_b', 'W1', 'b1', 'W2', 'b2')}
    del _L0_xattn_all

    def _L0_ffn_setup():
        import math
        import jax, jax.numpy as jnp
        import numpy as np
        B, T, D = (4, 1024, 256)
        H = 16
        HD = D // H
        CAP = int(1024 * 0.125)
        DFF = int(D * 4 * 2 / 3)
        EPS = 1e-06

        def rmsnorm(x, g):
            return x * jax.lax.rsqrt(jnp.mean(x * x, axis=-1, keepdims=True) + EPS) * g
        key = jax.random.key(seed)
        ks = jax.random.split(key, 9)
        s = lambda k, shape: jax.random.normal(k, shape, jnp.float32) * 0.02
        return {'x': jax.random.normal(ks[0], (B, T, D), jnp.float32), 'w_router': s(ks[1], (D,)), 'W_qkv': s(ks[2], (3 * D, D)), 'W_out': s(ks[3], (D, D)), 'g1': jnp.ones((D,), jnp.float32), 'g2': jnp.ones((D,), jnp.float32), 'W1': s(ks[4], (DFF, D)), 'W2': s(ks[5], (DFF, D)), 'W3': s(ks[6], (D, DFF))}
    _L0_ffn_all = _L0_ffn_setup()
    _L0_ffn_in = {k: v for k, v in _L0_ffn_all.items() if k in ('w_router', 'W_qkv', 'W_out', 'g1', 'g2', 'W1', 'W2', 'W3')}
    del _L0_ffn_all
    return {'x': x, 'ctx_1024': ctx_1024, 'L0_attn_w_attn': _L0_attn_in['w_attn'], 'L0_attn_w_proj': _L0_attn_in['w_proj'], 'L0_xattn_W_diff': _L0_xattn_in['W_diff'], 'L0_xattn_b_diff': _L0_xattn_in['b_diff'], 'L0_xattn_ln_g': _L0_xattn_in['ln_g'], 'L0_xattn_ln_b': _L0_xattn_in['ln_b'], 'L0_xattn_W1': _L0_xattn_in['W1'], 'L0_xattn_b1': _L0_xattn_in['b1'], 'L0_xattn_W2': _L0_xattn_in['W2'], 'L0_xattn_b2': _L0_xattn_in['b2'], 'L0_ffn_w_router': _L0_ffn_in['w_router'], 'L0_ffn_W_qkv': _L0_ffn_in['W_qkv'], 'L0_ffn_W_out': _L0_ffn_in['W_out'], 'L0_ffn_g1': _L0_ffn_in['g1'], 'L0_ffn_g2': _L0_ffn_in['g2'], 'L0_ffn_W1': _L0_ffn_in['W1'], 'L0_ffn_W2': _L0_ffn_in['W2'], 'L0_ffn_W3': _L0_ffn_in['W3']}

def reference(x, ctx_1024, L0_attn_w_attn, L0_attn_w_proj, L0_xattn_W_diff, L0_xattn_b_diff, L0_xattn_ln_g, L0_xattn_ln_b, L0_xattn_W1, L0_xattn_b1, L0_xattn_W2, L0_xattn_b2, L0_ffn_w_router, L0_ffn_W_qkv, L0_ffn_W_out, L0_ffn_g1, L0_ffn_g2, L0_ffn_W1, L0_ffn_W2, L0_ffn_W3):
    import jax
    import jax.numpy as jnp

    def _L0_attn_ref(x, w_attn, w_proj):
        import jax, jax.numpy as jnp
        import numpy as np
        N_HEAD = 16
        CHUNK = 128

        def _phi(x):
            return jax.nn.elu(x) + 1.0

        def _causal_linear_attn(qp, kp, v):
            B, H, T, D = qp.shape
            NC = T // CHUNK

            def to_chunks(a):
                return a.reshape(B, H, NC, CHUNK, D).transpose(2, 0, 1, 3, 4)
            qc, kc, vc = (to_chunks(qp), to_chunks(kp), to_chunks(v))
            mask = jnp.tril(jnp.ones((CHUNK, CHUNK), dtype=bool))

            def step(carry, blk):
                S, z = carry
                q_c, k_c, v_c = blk
                scores = jnp.einsum('bhcd,bhkd->bhck', q_c, k_c)
                scores = jnp.where(mask, scores, 0.0)
                num = jnp.einsum('bhck,bhke->bhce', scores, v_c) + jnp.einsum('bhcd,bhde->bhce', q_c, S)
                den = scores.sum(-1) + jnp.einsum('bhcd,bhd->bhc', q_c, z)
                S = S + jnp.einsum('bhkd,bhke->bhde', k_c, v_c)
                z = z + k_c.sum(axis=2)
                return ((S, z), (num, den))
            S0 = jnp.zeros((B, H, D, D), dtype=qp.dtype)
            z0 = jnp.zeros((B, H, D), dtype=qp.dtype)
            _, (num, den) = jax.lax.scan(step, (S0, z0), (qc, kc, vc))
            y = num / (den[..., None] + 1e-06)
            y = y.transpose(1, 2, 0, 3, 4).reshape(B, H, T, D)
            return y
        B, T, E = x.shape
        H = N_HEAD
        D = E // H
        qkv = x @ w_attn.T
        q, k, v = jnp.split(qkv, 3, axis=2)

        def heads(a):
            return a.reshape(B, T, H, D).transpose(0, 2, 1, 3)
        y = _causal_linear_attn(_phi(heads(q)), _phi(heads(k)), heads(v))
        y = y.transpose(0, 2, 1, 3).reshape(B, T, E)
        return y @ w_proj.T

    def _L0_xattn_ref(q, k, v, W_diff, b_diff, ln_g, ln_b, W1, b1, W2, b2):
        import jax, jax.numpy as jnp
        import numpy as np
        EPS = 1e-08
        LN_EPS = 1e-05

        def _layernorm(x, g, b):
            mu = jnp.mean(x, axis=-1, keepdims=True)
            var = jnp.var(x, axis=-1, keepdims=True)
            return (x - mu) * jax.lax.rsqrt(var + LN_EPS) * g + b

        def _prob(x):
            x = jnp.tanh(x) * 0.499 + 0.5
            return jnp.clip(x / (jnp.sum(x, axis=-1, keepdims=True) + EPS), EPS)
        D = q.shape[-1]
        q_prob = _prob(q)
        k_prob = _prob(k)
        log_ratio = jnp.log(q_prob) - jnp.log(k_prob)
        sid = jnp.einsum('bnd,bmd->bnm', q_prob - k_prob, log_ratio)
        sid_sim = -sid
        attn = jax.nn.softmax(sid_sim / D ** 0.5, axis=-1)
        attn_feat = jnp.einsum('bnm,bmd->bnd', attn, v)
        f_diff = (v - attn_feat) @ W_diff.T + b_diff + q
        h = _layernorm(f_diff, ln_g, ln_b)
        mlp = jax.nn.gelu(h @ W1.T + b1, approximate=False) @ W2.T + b2
        out = mlp + f_diff
        return _layernorm(out, ln_g, ln_b)

    def _L0_ffn_ref(x, w_router, W_qkv, W_out, g1, g2, W1, W2, W3):
        import math
        import jax, jax.numpy as jnp
        import numpy as np
        B, T, D = (4, 1024, 256)
        H = 16
        HD = D // H
        CAP = int(1024 * 0.125)
        DFF = int(D * 4 * 2 / 3)
        EPS = 1e-06

        def rmsnorm(x, g):
            return x * jax.lax.rsqrt(jnp.mean(x * x, axis=-1, keepdims=True) + EPS) * g
        Bq, Tq, Dq = x.shape
        scores = x @ w_router
        _, idx = jax.lax.top_k(scores, CAP)
        x_sel = jnp.take_along_axis(x, idx[:, :, None], axis=1)
        h = rmsnorm(x_sel, g1)
        qkv = (h @ W_qkv.T).reshape(Bq, CAP, 3, H, HD)
        q, k, v = jnp.moveaxis(qkv, 2, 0)
        att = jnp.einsum('bqhd,bkhd->bhqk', q, k) / math.sqrt(HD)
        mask = jnp.triu(jnp.ones((CAP, CAP), bool), 1)
        att = jnp.where(mask, -jnp.inf, att)
        att = jax.nn.softmax(att, axis=-1)
        o = jnp.einsum('bhqk,bkhd->bqhd', att, v).reshape(Bq, CAP, Dq)
        x_attn = o @ W_out.T
        h2 = rmsnorm(x_sel + x_attn, g2)
        x_ff = jax.nn.silu(h2 @ W1.T) * (h2 @ W2.T) @ W3.T
        x_proc = x_sel + x_attn + x_ff
        out = x.at[jnp.arange(Bq)[:, None], idx].set(x_proc)
        return out
    x = x + _L0_attn_ref(_layernorm(x, axis=-1), L0_attn_w_attn, L0_attn_w_proj)
    x = x + _L0_xattn_ref(_layernorm(x, axis=-1), ctx_1024, ctx_1024, L0_xattn_W_diff, L0_xattn_b_diff, L0_xattn_ln_g, L0_xattn_ln_b, L0_xattn_W1, L0_xattn_b1, L0_xattn_W2, L0_xattn_b2)
    x = x + _L0_ffn_ref(_layernorm(x, axis=-1), L0_ffn_w_router, L0_ffn_W_qkv, L0_ffn_W_out, L0_ffn_g1, L0_ffn_g2, L0_ffn_W1, L0_ffn_W2, L0_ffn_W3)
    return x

_drawn_inputs = setup_inputs


def setup_inputs(seed=0):
    import zlib

    import numpy as np

    out = dict(_drawn_inputs(seed))
    spreads = {'L0_xattn_b_diff': (0.0, 0.1),
     'L0_xattn_ln_g': (1.0, 0.2),
     'L0_xattn_ln_b': (0.0, 0.1),
     'L0_xattn_b1': (0.0, 0.474),
     'L0_xattn_b2': (0.0, 0.1),
     'L0_ffn_g1': (1.0, 0.6),
     'L0_ffn_g2': (1.0, 0.6)}
    factors = {'L0_attn_w_attn': 3.541,
     'L0_attn_w_proj': 3.514,
     'L0_ffn_w_router': 7.645,
     'L0_ffn_W_qkv': 8.0,
     'L0_ffn_W_out': 8.0,
     'L0_ffn_W1': 8.0,
     'L0_ffn_W2': 8.0,
     'L0_ffn_W3': 8.0}
    for name, (base, spread) in spreads.items():
        noise = np.random.default_rng([zlib.crc32(name.encode()), seed]).standard_normal(out[name].shape)
        drawn = base * np.exp(spread * noise) if base else spread * noise
        out[name] = jnp.asarray(drawn.astype(out[name].dtype))
    for name, factor in factors.items():
        out[name] = (out[name] * factor).astype(out[name].dtype)
    return out
```

```python
from contextlib import ExitStack

import numpy as np

import concourse.bass as bass
from concourse import mybir

F32 = mybir.dt.float32
F32R = mybir.dt.float32r
BF16 = mybir.dt.bfloat16
ALU = mybir.AluOpType
ACT = mybir.ActivationFunctionType
AX = mybir.AxisListType

B, T, D = 16, 256, 256
P = 128
TT = T // P
DC = D // P
NH, HD = 16, 16
R = 128
MLP = 1024
FF = 682
FFP = 768
FG = 342
LN_EPS, RMS_EPS, DEN_EPS, PROB_EPS = 1e-5, 1e-6, 1e-6, 1e-8
NEG = -3.0e38
NRAW = 3
ROW = D * TT

CONST = {}
_at = 0
for _name, _n in (("ident2", TT * T), ("tri_ones", T), ("neg_mask", P), ("head_block", P),
                  ("tie_mask", TT * T), ("iota", 1), ("even", 1), ("odd", 1), ("even4", 1), ("odd4", 1),
                  ("minus_half", TT), ("prob_bias", 1)):
    CONST[_name] = slice(_at, _at + _n)
    _at += _n
NCONST = _at

ORDER = ["A1", "B1", "C1", "A2", "C2", "B1k", "A1k", "B2", "A3", "C3", "A3b", "B3", "C4", "B3b", "A4", "C5_0", "A4b", "B4", "C5_1",
         "B5", "A5_0", "C5_2", "A5_1", "B6", "C5_3", "A5_2", "B7", "C5_4", "A5_3", "C6", "B8_0", "A5_4", "B8_1",
         "C6b", "A5_5", "B8_2", "A5_6", "B8_3", "A5_7", "B9", "A5_8", "C7_0", "B9b", "C7_1", "A6", "C8", "C8b"]
SKEW = {"A": 0, "B": 1, "C": 2}


class Signal:

    def __init__(self, sem, per_row):
        self.sem, self.per_row = sem, per_row

    def __call__(self, b, k=None):
        return self.sem, b * self.per_row + (self.per_row if k is None else k)


def first(b):
    return isinstance(b, int) and b == 0


def rounds(eng, steps, before=(lambda: None,) * 3):
    def one(i, on):
        for name in ORDER:
            if name[0] in on and name in steps:
                steps[name](i - SKEW[name[0]])
    before[0]()
    one(0, "A")
    before[1]()
    one(1, "AB")
    before[2]()
    one(2, "ABC")
    with eng.Fori(3, B) as i:
        one(i, "ABC")
    one(B, "BC")
    one(B + 1, "C")


def decoder(nc, x, ctx_in, consts, vec_bc, vec_cols, w_a, w_proj, w_diff, w_1, w_2, w_cqk, w_cv, w_out, w_gu, w_3, out):
    ctx = ExitStack()
    with ctx:
        def sb(name, shape, dt=F32):
            return ctx.enter_context(nc.sbuf_tensor(name, shape, dt))

        def sig(name, per_row=1):
            return Signal(ctx.enter_context(nc.semaphore(name)), per_row)

        const = sb("const", [P, NCONST])
        C = {n: const[:, s] for n, s in CONST.items()}
        tri, neg_mask = C["tri_ones"][:, 0:P], C["neg_mask"]
        ident2 = C["ident2"].rearrange("p (t n) -> p t n", t=TT)
        ident = ident2[:, 0, 0:P]
        tie_mask = C["tie_mask"].rearrange("p (t n) -> p t n", t=TT)
        ones_bf = sb("ones_bf", [P, P], BF16)
        bc = sb("vectors_by_row", [P, 5, D])
        ln_g_bc, ln_b_bc, b2_bc, b_diff_bc, router_bc = (bc[:, n, :] for n in range(5))
        cols = sb("vectors_by_column", [P, 4 * DC + MLP // P])
        ln_g_col, ln_b_col, g1_col, g2_col = (cols[:, n * DC:(n + 1) * DC] for n in range(4))
        b1_col = cols[:, 4 * DC:]

        def pair(name, shape):
            return sb(name + "_hi", shape, F32R), sb(name + "_lo", shape, F32R)

        wa = pair("w_attn", [P, DC, 3 * D])
        wp = pair("w_proj", [P, DC, D])
        wd = pair("w_diff", [P, DC, D])
        w1 = pair("w_mlp1", [P, DC, MLP])
        w2 = pair("w_mlp2", [P, MLP // P, D])
        wcv = pair("w_ffn_v", [P, DC, D])
        wo = pair("w_ffn_out", [P, DC, D])
        wgu = pair("w_ffn_gu", [P, DC, 2 * FF])
        w3 = pair("w_ffn_3", [P, FFP // P, D])
        wcqk = sb("w_ffn_qk", [P, DC, 2 * D])

        xin = sb("x_in", [P, TT, D])
        a_norm = sb("a_norm", [P, TT, D])
        a_tr = pair("a_tr", [P, DC, T])
        a_e0 = sb("a_e0", [P, 512])
        a_e1 = sb("a_e1", [P, 512])
        a_s1 = sb("a_s1", [P, 512])
        qT = sb("qT", [P, DC, T])
        qM = [sb("qT_even", [P, DC, T]), sb("qT_odd", [P, DC, T])]
        kT = sb("kT", [P, DC, T])
        k_tok = sb("k_tok", [P, TT, D])
        vM = [sb("v_even", [P, TT, D]), sb("v_odd", [P, TT, D])]
        v0 = sb("v_first", [P, D])
        state = sb("state", [P, D])
        x1 = sb("x1", [P, TT, D])
        a_st = sb("a_st", [P, TT, 6])
        a_mv = sb("a_mv", [P, TT, 2])
        a_rs = sb("a_rs", [P, TT])

        qc = sb("qc", [P, 2 * TT, D])
        prob = sb("prob", [P, 2 * TT, D])
        b_f0 = sb("b_f0", [P, TT, D])
        b_f1 = sb("b_f1", [P, TT, D])
        b_s0 = pair("b_s0", [P, 512])
        b_s1 = pair("b_s1", [P, 512])
        b_s2 = pair("b_s2", [P, 512])
        qb = sb("q_bias", [P, TT, D])
        x2 = sb("x2", [P, TT, D])
        b_st = sb("b_st", [P, TT, 6])
        b_mv = sb("b_mv", [P, TT, 2])
        b_rs = sb("b_rs", [P, TT])
        b_sum = sb("b_sum", [P, 2 * TT])
        b_rsum = sb("b_rsum", [P, 2 * TT])
        b_min = sb("b_min", [P, TT])
        b_bias = sb("b_bias", [P, TT])
        b_z = sb("b_z", [P, TT])
        b_nz = sb("b_nz", [P, TT])

        raw = sb("w_raw_or_stage_c", [P, NRAW, MLP])
        parts = [raw[:, n // 2, n % 2 * ROW:(n % 2 + 1) * ROW] for n in range(5)]
        c_norm = parts[0].rearrange("p (t d) -> p t d", t=TT)
        c_pre = parts[1].rearrange("p (t d) -> p t d", t=TT)
        ob = parts[2].rearrange("p (t d) -> p t d", t=TT)
        c_et = parts[3:5]
        before = sb("before", [P, TT, T], BF16)
        tie = sb("tie", [P, T])
        sel_t = sb("select_by_rank", [P, T], F32R)
        sel = sb("select_by_token", [P, TT, R])
        c_hT = sb("c_hT", [P, DC, R])
        c_hs = pair("c_hs", [P, DC, R])
        x_sel = sb("x_sel", [P, D])
        cq = [sb("c_q_even", [P, DC, R]), sb("c_q_odd", [P, DC, R])]
        ck = sb("c_k", [P, DC, R])
        cv = [sb("c_v_even", [P, D]), sb("c_v_odd", [P, D])]
        c_max = sb("c_max", [P, NH])
        c_den = sb("c_den", [P, NH])
        x_att = sb("x_att", [P, D])
        c_rT = x_att
        c_h2 = sb("c_h2", [P, D])
        c_h2n = sb("c_h2n", [P, D])
        c_rden = c_h2n
        act = sb("gated", [P, FFP])
        act_t = pair("gated_t", [P, FFP // P, R])
        c_st = sb("c_st", [P, TT, 6])
        c_mv = sb("c_mv", [P, TT, 2])
        c_rs = sb("c_rs", [P, TT])
        c_sc = sb("c_sc", [P, TT])
        c_sq = sb("c_sq", [P, TT])
        c_rms = sb("c_rms", [P, TT])
        c_sq2 = sb("c_sq2", [P, 1])
        c_rms2 = sb("c_rms2", [P, 1])


        bank = [ctx.enter_context(nc.psum_tensor(f"bank{n}", [P, 512], F32)) for n in range(8)]
        a0, a1, a2, b0, b1, c0, c1, c2 = bank

        loads = [
            *[(w_a[:, k, :], 3 * D, (wa[0][:, k, :], wa[1][:, k, :])) for k in range(DC)],
            (w_proj, DC * D, tuple(w[:, :, :].rearrange("p k n -> p (k n)") for w in wp)),
            (w_diff, DC * D, tuple(w[:, :, :].rearrange("p k n -> p (k n)") for w in wd)),
            *[(w_1[:, k, :], MLP, (w1[0][:, k, :], w1[1][:, k, :])) for k in range(DC)],
            *[(w_2[:, 4 * k:4 * k + 4, :].rearrange("p k n -> p (k n)"), 4 * D,
               tuple(w[:, 4 * k:4 * k + 4, :].rearrange("p k n -> p (k n)") for w in w2)) for k in range(2)],
            (w_cv, DC * D, tuple(w[:, :, :].rearrange("p k n -> p (k n)") for w in wcv)),
            (w_out, DC * D, tuple(w[:, :, :].rearrange("p k n -> p (k n)") for w in wo)),
            *[(w_gu[:, k, h * FF:(h + 1) * FF], FF, tuple(w[:, k, h * FF:(h + 1) * FF] for w in wgu))
              for k in range(DC) for h in range(2)],
            *[(w_3[:, 3 * k:3 * k + 3, :].rearrange("p k n -> p (k n)"), 3 * D,
               tuple(w[:, 3 * k:3 * k + 3, :].rearrange("p k n -> p (k n)") for w in w3)) for k in range(2)],
        ]
        LOADS_A, LOADS_B = 3, 5

        const_in, vec_in, qk_in = sig("const_in"), sig("vec_in"), sig("qk_in")
        raw_in = [sig(f"raw_in{n}") for n in range(NRAW)]
        raw_hi, raw_lo, ones_set, v_zero = sig("raw_hi"), sig("raw_lo"), sig("ones_set"), sig("v_zero")
        x_in, ctx_in_s, out_done = sig("x_loaded", 16), sig("ctx_loaded", 16), sig("out_stored", 16)
        a_mean, a_rstd, a_normed = sig("a_mean", 2 * TT), sig("a_rstd", 2), sig("a_normed", TT)
        x_kept, a_tp, a_thi, a_tlo = sig("x_kept"), sig("a_tp"), sig("a_thi"), sig("a_tlo")
        qk_mm, q_out, k_out = sig("qk_mm", 2), sig("q_out", 2), sig("k_out", 2)
        qk_phi, q_mask = sig("qk_phi", 2), sig("q_mask", 2)
        kv_mm, kv_out, kv_phi, v_put = (sig("kv_mm", TT), sig("kv_out", 2 * TT), sig("kv_phi", TT), sig("v_put", 2 * TT + 1))
        s_mm, ksum_mm, s_put, ksum_q, den_mm, den_inv = (
            sig("s_mm"), sig("ksum_mm"), sig("s_put"), sig("ksum_q"), sig("den_mm"), sig("den_inv", 2))
        score_mm, score_put, av_mm = sig("score_mm", 8), sig("score_put", 8), sig("av_mm", 8)
        y_put, y_hi, y_lo, proj_mm, a_done = sig("y_put"), sig("y_hi"), sig("y_lo"), sig("proj_mm"), sig("a_done")

        b_mean, b_rstd, q_normed = sig("b_mean", 2 * TT), sig("b_rstd", 2), sig("q_normed", TT)
        x1_kept, qb_put, c_hi, c_lo = sig("x1_kept"), sig("qb_put"), sig("ctx_hi"), sig("ctx_lo")
        p_exp, p_inv, p_raw, p_rsum, p_norm = (sig("p_exp"), sig("p_inv", 2), sig("p_raw", 4), sig("p_rsum", 2),
                                               sig("p_norm", 4))
        diff_put, p_log, ratio_put = sig("diff_put"), sig("p_log"), sig("ratio_put")
        dr_tp, dr_hi, dr_lo = sig("dr_tp", 2), sig("dr_hi", 2), sig("dr_lo", 2)
        sid_mm, sid_bias, sid_exp, z_neg, att_put = (
            sig("sid_mm"), sig("sid_bias", 2), sig("sid_exp", TT), sig("z_neg", 2), sig("att_put", TT))
        att_tp, att_hi, att_lo, fd_mm, fd_hi, fd_lo, f_mm, f_put = (
            sig("att_tp"), sig("att_hi"), sig("att_lo"), sig("fd_mm"), sig("fd_hi"), sig("fd_lo"), sig("f_mm"),
            sig("f_put"))
        f_mean, f_rstd, f_normed, f_kept = sig("f_mean", 2 * TT), sig("f_rstd", 2), sig("f_normed", TT), sig("f_kept")
        h_tp, h_aff, h_hi, h_lo = sig("h_tp"), sig("h_aff", DC), sig("h_hi"), sig("h_lo")
        up_mm, gelu_put, g_hi, g_lo, down_mm = (sig("up_mm", 4), sig("gelu_put", 8), sig("g_hi", 4), sig("g_lo", 4),
                                                sig("down_mm", 4))
        o_put, o_mean, o_rstd, o_normed, o_gain, b_done = (
            sig("o_put"), sig("o_mean", 2 * TT), sig("o_rstd", 2), sig("o_normed", TT), sig("o_gain"), sig("b_done"))

        c_mean, c_rstd, c_normed, ob_put = sig("c_mean", 2 * TT), sig("c_rstd", 2), sig("c_normed", TT), sig("ob_put")
        r_score, r_sq, r_rms, pre_put = sig("r_score", TT), sig("r_sq", TT), sig("r_rms", 2), sig("pre_put", TT)
        sc_bc, before_put, rank_mm, selt_put, sel_tp, sel_put = (
            sig("sc_bc"), sig("before_put", 2 * TT), sig("rank_mm"), sig("selt_put"), sig("sel_tp"),
            sig("sel_put"))
        hg_mm, xs_mm, xs_put, hg_put, hg_hi, hg_lo = (sig("hg_mm"), sig("xs_mm"), sig("xs_put"), sig("hg_put", DC),
                                                      sig("hg_hi"), sig("hg_lo"))
        cqk_mm, cv_mm, cqk_put, cv_put = sig("cqk_mm"), sig("cv_mm"), sig("cqk_put", 3), sig("cv_put", 2)
        cs_mm, cs_max, cs_sub, cs_exp, cs_sum, cs_tp, cs_et, cav_mm = (
            sig("cs_mm", 4), sig("cs_max", 8), sig("cs_sub", 4), sig("cs_exp", 4), sig("cs_sum", 4),
            sig("cs_tp", 4), sig("cs_et", 4), sig("cav_mm", 4))
        cden_bc, cden_tp, cden_put, co_put, co_hi, co_lo = (
            sig("cden_bc", 3), sig("cden_tp"), sig("cden_put"), sig("co_put"), sig("co_hi"),
            sig("co_lo"))
        xo_mm, xo_put, h2_sum, h2_sq, h2_rms, h2_norm, h2_tp, h2_put, h2_hi, h2_lo = (
            sig("xo_mm"), sig("xo_put"), sig("h2_sum"), sig("h2_sq"), sig("h2_rms", 2), sig("h2_norm"),
            sig("h2_tp"), sig("h2_put", DC), sig("h2_hi"), sig("h2_lo"))
        gu_mm, g_exp, g_inv, g_gate, g_act = (sig("gu_mm", 2), sig("g_exp", 2), sig("g_inv", 4),
                                                     sig("g_gate", 2), sig("g_act", 2))
        at_tp, at_hi, at_lo, ff_mm, ff_put, ff_hi, ff_lo, scat_mm, c_done = (
            sig("at_tp", 2), sig("at_hi", 2), sig("at_lo", 2), sig("ff_mm"), sig("ff_put"), sig("ff_hi"),
            sig("ff_lo"), sig("scat_mm"), sig("c_done"))

        passed = sig("passed")

        def rows_of(t):
            return t.rearrange("(b t p) d -> b p t d", b=B, p=P)

        x_rows, ctx_rows, out_rows = rows_of(x), rows_of(ctx_in), rows_of(out)

        block = ctx.enter_context(nc.Block())

        @block.sync
        def _(sp):
            sp.dma_start(const[:, :], consts).then_inc(const_in.sem, 16)
            sp.dma_start(xin[:, :, :], x_rows[0]).then_inc(x_in.sem, 16)

            def load_weights(lo, hi):
                for n in range(lo, hi):
                    if n >= NRAW:
                        sp.wait_ge(raw_hi.sem, n - NRAW + 1)
                        sp.wait_ge(raw_lo.sem, n - NRAW + 1)
                    sp.dma_start(raw[:, n % NRAW, 0:loads[n][1]], loads[n][0]).then_inc(raw_in[n % NRAW].sem, 16)

            load_weights(0, LOADS_A)
            sp.dma_start(bc[:, :, :], vec_bc).then_inc(vec_in.sem, 16)
            sp.dma_start(cols[:, :], vec_cols).then_inc(vec_in.sem, 16)
            sp.dma_start(qc[:, TT:2 * TT, :], ctx_rows[0]).then_inc(ctx_in_s.sem, 16)
            sp.dma_start(wcqk[:, :, :], w_cqk).then_inc(qk_in.sem, 16)

            def next_x(b):
                sp.wait_ge(*a_normed(b))
                sp.sem_inc(passed.sem, 1)
                sp.wait_ge(*x_kept(b))
                sp.sem_inc(passed.sem, 1)
                sp.dma_start(xin[:, :, :], x_rows[b + 1]).then_inc(x_in.sem, 16)

            def next_ctx(b):
                sp.wait_ge(*p_exp(b))
                sp.wait_ge(*c_hi(b))
                sp.wait_ge(*c_lo(b))
                sp.sem_inc(passed.sem, 1)
                sp.dma_start(qc[:, TT:2 * TT, :], ctx_rows[b + 1]).then_inc(ctx_in_s.sem, 16)

            def store(b):
                sp.wait_ge(*c_done(b))
                sp.sem_inc(passed.sem, 1)
                sp.dma_start(out_rows[b], ob[:, :, :]).then_inc(out_done.sem, 16)

            next_x(0)
            load_weights(LOADS_A, LOADS_A + LOADS_B + NRAW)
            next_x(1)
            next_ctx(0)
            load_weights(LOADS_A + LOADS_B + NRAW, len(loads))
            next_x(2)
            next_ctx(1)
            store(0)
            with sp.Fori(3, B - 1) as i:
                next_x(i)
                next_ctx(i - 1)
                store(i - 2)
            next_ctx(B - 2)
            store(B - 3)
            store(B - 2)
            store(B - 1)
            sp.wait_ge(*out_done(B - 1))

        @block.gpsimd
        def _(pool):
            nc.gpsimd.memset(ones_bf[:, :], 1.0).then_inc(ones_set.sem, 1)
            pool.wait_ge(const_in.sem, 16)

            def power(mean_done, b, var, eps, scale, out_, rstd_done, n):
                pool.wait_ge(*mean_done(b))
                pool.sem_inc(passed.sem, 1)
                nc.gpsimd.tensor_scalar(out_, var, scale, eps, ALU.mult, ALU.add).then_inc(rstd_done.sem, 1)
                pool.wait_ge(*rstd_done(b, 1))
                nc.gpsimd.tensor_tensor(out_, out_, C["minus_half"][:, 0:n], ALU.pow).then_inc(rstd_done.sem, 1)

            def a1_(b):
                power(a_mean, b, a_mv[:, :, 1], LN_EPS, 1.0, a_rs[:, :], a_rstd, TT)

            def a1k_(b):
                if not first(b):
                    pool.wait_ge(*x1_kept(b - 1))
                    pool.wait_ge(*q_normed(b - 1))
                pool.wait_ge(*x_in(b))
                pool.sem_inc(passed.sem, 1)
                nc.gpsimd.tensor_copy(x1[:, :, :], xin[:, :, :]).then_inc(x_kept.sem, 1)

            def b1_(b):
                power(b_mean, b, b_mv[:, :, 1], LN_EPS, 1.0, b_rs[:, :], b_rstd, TT)

            def b1k_(b):
                pool.wait_ge(*a_done(b))
                if not first(b):
                    pool.wait_ge(*ob_put(b - 1))
                    pool.wait_ge(*c_normed(b - 1))
                else:
                    pool.wait_ge(vec_in.sem, 32)
                nc.gpsimd.tensor_tensor(x2[:, :, :], x1[:, :, :], ln_b_bc.unsqueeze(1).broadcast_to([P, TT, D]),
                                        ALU.add).then_inc(x1_kept.sem, 1)

            def b2_(b):
                pool.wait_ge(*c_hi(b))
                nc.gpsimd.tensor_tensor(b_s2[1][:, :], qc[:, TT:2 * TT, :].rearrange("p t d -> p (t d)"),
                                        b_s2[0][:, :].bitcast(F32), ALU.subtract).then_inc(c_lo.sem, 1)
                pool.wait_ge(*q_normed(b))
                nc.gpsimd.tensor_tensor(qb[:, :, :], qc[:, 0:TT, :],
                                        b_diff_bc.unsqueeze(1).broadcast_to([P, TT, D]), ALU.add).then_inc(qb_put.sem, 1)

            def b7_(b):
                power(f_mean, b, b_mv[:, :, 1], LN_EPS, 1.0, b_rs[:, :], f_rstd, TT)
                nc.gpsimd.tensor_tensor(qb[:, :, :], b_f0[:, :, :], b2_bc.unsqueeze(1).broadcast_to([P, TT, D]),
                                        ALU.add).then_inc(f_kept.sem, 1)

            def b9b_(b):
                power(o_mean, b, b_mv[:, :, 1], LN_EPS, 1.0, b_rs[:, :], o_rstd, TT)

            def c1_(b):
                power(c_mean, b, c_mv[:, :, 1], LN_EPS, 1.0, c_rs[:, :], c_rstd, TT)

            def c2_(b):
                power(r_sq, b, c_sq[:, :], RMS_EPS, 1.0 / D, c_rms[:, :], r_rms, TT)
                pool.wait_ge(*c_normed(b))
                if not first(b):
                    pool.wait_ge(*out_done(b - 1))
                nc.gpsimd.tensor_tensor(ob[:, :, :], x2[:, :, :], c_norm[:, :, :], ALU.add).then_inc(ob_put.sem, 1)

            def c_sub(g):
                def step(b):
                    logits = (c_norm, c_pre)[g % 2][:, :, :].rearrange("p t d -> p (t d)") \
                        .rearrange("p (h k) -> p h k", h=4)
                    pool.wait_ge(*cs_max(b, 2 * g + 2))
                    nc.gpsimd.tensor_tensor(logits, logits, c_max[:, 4 * g:4 * g + 4].unsqueeze(2)
                                            .broadcast_to([P, 4, R]), ALU.subtract).then_inc(cs_sub.sem, 1)
                return step

            def c6b_(b):
                power(h2_sq, b, c_sq2[:, :], RMS_EPS, 1.0 / D, c_rms2[:, :], h2_rms, 1)

            rounds(pool, {"A1": a1_, "A1k": a1k_, "B1": b1_, "B1k": b1k_, "B2": b2_, "B7": b7_, "B9b": b9b_, "C1": c1_, "C2": c2_,
                          **{f"C5_{g}": c_sub(g) for g in range(4)}, "C6": c6b_})

        @block.scalar
        def _(act_e):
            act_in = nc.scalar.activation

            def copy(out_, in_, done):
                act_in(out_, in_, ACT.Copy).then_inc(done.sem, 1)

            def split_weights(lo, hi):
                for n in range(lo, hi):
                    act_e.wait_ge(raw_in[n % NRAW].sem, 16 * (n // NRAW + 1))
                    copy(loads[n][2][0], raw[:, n % NRAW, 0:loads[n][1]], raw_hi)

            def a2_(b):
                act_e.wait_ge(*a_tp(b))
                copy(a_tr[0][:, :, :].rearrange("p c t -> p (c t)"), a0[:, :], a_thi)

            def a3_(b):
                act_e.wait_ge(*qk_mm(b, 1))
                act_in(a_e0[:, :], a1[:, :], ACT.Exp).then_inc(q_out.sem, 1)
                act_in(qT[:, :, :].rearrange("p c t -> p (c t)"), a1[:, :], ACT.Relu).then_inc(q_out.sem, 1)
                act_e.wait_ge(*qk_mm(b, 2))
                act_in(a_e1[:, :], a2[:, :], ACT.Exp).then_inc(k_out.sem, 1)
                act_in(kT[:, :, :].rearrange("p c t -> p (c t)"), a2[:, :], ACT.Relu).then_inc(k_out.sem, 1)

            def a3b_(b):
                for t, bk in enumerate((a0, a1)):
                    act_e.wait_ge(*kv_mm(b, t + 1))
                    act_in(a_s1[:, t * D:(t + 1) * D], bk[:, 0:D], ACT.Exp).then_inc(kv_out.sem, 1)
                    act_in(k_tok[:, t, :], bk[:, 0:D], ACT.Relu).then_inc(kv_out.sem, 1)
                act_e.wait_ge(*qk_phi(b, 1))
                for m, mask in enumerate(("even", "odd")):
                    act_in(qM[m][:, :, :], qT[:, :, :], ACT.Copy, scale=C[mask]).then_inc(q_mask.sem, 1)

            def a6_(b):
                act_e.wait_ge(*y_put(b))
                copy(a_tr[0][:, :, :], a_norm[:, :, :], y_hi)

            def b1_(b):
                act_e.wait_ge(*ctx_in_s(b))
                copy(b_s2[0][:, :], qc[:, TT:2 * TT, :].rearrange("p t d -> p (t d)"), c_hi)

            def b2_(b):
                act_e.wait_ge(*q_normed(b))
                act_in(prob[:, :, :], qc[:, :, :], ACT.Exp, scale=2.0).then_inc(p_exp.sem, 1)
                act_e.wait_ge(*p_inv(b))
                for s in range(2 * TT):
                    act_in(prob[:, s, :], prob[:, s, :], ACT.Identity, bias=C["prob_bias"], scale=-0.998,
                           accum_out=b_sum[:, s:s + 1]).then_inc(p_raw.sem, 1)
                act_e.wait_ge(*diff_put(b))
                act_in(prob[:, :, :], prob[:, :, :], ACT.Ln).then_inc(p_log.sem, 1)

            def b3_(b):
                act_e.wait_ge(*dr_tp(b, 1))
                copy(b_s0[0][:, :], b0[:, :], dr_hi)
                act_e.wait_ge(*dr_tp(b, 2))
                copy(b_s1[0][:, :], b1[:, :], dr_hi)

            def b4_(b):
                act_e.wait_ge(*sid_bias(b))
                for t in range(TT):
                    act_in(prob[:, t, :], b0[:, t * T:(t + 1) * T], ACT.Exp, bias=b_bias[:, t:t + 1],
                           scale=-1.0 / D ** 0.5, accum_out=b_z[:, t:t + 1]).then_inc(sid_exp.sem, 1)

            def b5_(b):
                act_e.wait_ge(*att_tp(b))
                copy(b_s0[0][:, :], b1[:, :], att_hi)

            def b6_(b):
                act_e.wait_ge(*fd_mm(b))
                copy(b_s1[0][:, :], b0[:, :], fd_hi)

            def b7_(b):
                act_e.wait_ge(*h_aff(b))
                copy(b_s0[0][:, :], b_f1[:, :, :].rearrange("p c t -> p (c t)"), h_hi)

            def gelu(j):
                def step(b):
                    act_e.wait_ge(*up_mm(b, j + 1))
                    if j >= 2:
                        act_e.wait_ge(*g_lo(b, j - 1))
                    for n in range(2):
                        f = 2 * j + n
                        act_in(prob[:, 2 * (j % 2) + n, :], b0[:, n * T:(n + 1) * T], ACT.Gelu,
                               bias=b1_col[:, f:f + 1]).then_inc(gelu_put.sem, 1)
                return step

            def c1_(b):
                act_e.wait_ge(*c_normed(b))
                for t in range(TT):
                    act_in(c_h2n[:, :], c_norm[:, t, :], ACT.Square, accum_out=c_sq[:, t:t + 1]).then_inc(r_sq.sem, 1)
                    act_e.wait_ge(*r_sq(b, t + 1))

            def c2_(b):
                act_e.wait_ge(*r_rms(b))
                for t in range(TT):
                    act_in(c_pre[:, t, :], c_norm[:, t, :], ACT.Copy, scale=c_rms[:, t:t + 1]).then_inc(pre_put.sem, 1)

            def c3_(b):
                act_e.wait_ge(*sel_tp(b))
                copy(sel[:, :, :].rearrange("p t r -> p (t r)"), c2[:, 0:T], sel_put)

            def c4_(b):
                act_e.wait_ge(*xs_mm(b))
                copy(x_sel[:, :], c1[:, 0:D], xs_put)
                act_e.wait_ge(*hg_put(b))
                copy(c_hs[0][:, :, :], c_hT[:, :, :], hg_hi)
                act_e.wait_ge(*cqk_mm(b))
                for m, mask in enumerate(("even4", "odd4")):
                    act_in(cq[m][:, :, :].rearrange("p c r -> p (c r)"), c2[:, 0:2 * R], ACT.Copy, scale=C[mask]) \
                        .then_inc(cqk_put.sem, 1)
                copy(ck[:, :, :].rearrange("p c r -> p (c r)"), c2[:, 2 * R:4 * R], cqk_put)

            def c_exp(g):
                def step(b):
                    logits = (c_norm, c_pre)[g % 2]
                    act_e.wait_ge(*cs_sub(b, g + 1))
                    act_in(logits[:, :, :], logits[:, :, :], ACT.Exp).then_inc(cs_exp.sem, 1)
                    if g >= 1:
                        c_et_put(b, g - 1)
                return step

            def c_et_put(b, g):
                act_e.wait_ge(*cs_tp(b, g + 1))
                copy(c_et[g % 2][:, :], (c1, c2)[g % 2][:, :], cs_et)

            def c5_4(b):
                c_et_put(b, 3)
                act_e.wait_ge(*cden_tp(b))
                copy(c_rT[:, :], c0[:, D:2 * D], cden_put)

            def c6_(b):
                act_e.wait_ge(*co_put(b))
                copy(c_hs[0][:, :, :], c_hT[:, :, :], co_hi)
                act_e.wait_ge(*xo_mm(b))
                copy(x_att[:, :], c0[:, 0:D], xo_put)
                act_e.wait_ge(*h2_sum(b))
                act_in(c_h2n[:, :], c_h2[:, :], ACT.Square, accum_out=c_sq2[:, :]).then_inc(h2_sq.sem, 1)

            def c6b_(b):
                act_e.wait_ge(*h2_put(b))
                copy(c_hs[0][:, :, :], c_hT[:, :, :], h2_hi)

            def c7(j):
                def step(b):
                    n = (FG, FF - FG)[j]
                    act_e.wait_ge(*gu_mm(b, j + 1))
                    if j:
                        act_e.wait_ge(*g_gate(b, 1))
                    act_in(c_et[0][:, 0:n], c1[:, 0:n], ACT.Exp, scale=-1.0).then_inc(g_exp.sem, 1)
                return step

            def c8_(b):
                for j, (bk, s) in enumerate(((c1, slice(0, 4)), (c2, slice(4, 6)))):
                    act_e.wait_ge(*at_tp(b, j + 1))
                    n = (s.stop - s.start) * R
                    copy(act_t[0][:, s, :].rearrange("p c r -> p (c r)"), bk[:, 0:n], at_hi)

            def c8b_(b):
                act_e.wait_ge(*ff_put(b))
                copy(c_hs[0][:, :, :].rearrange("p c r -> p (c r)"), c_h2[:, :], ff_hi)

            act_e.wait_ge(const_in.sem, 16)

            def before_b():
                split_weights(LOADS_A, LOADS_A + LOADS_B)
                act_e.wait_ge(vec_in.sem, 32)

            rounds(act_e, {"A2": a2_, "A3": a3_, "A3b": a3b_, "A6": a6_, "B1": b1_, "B2": b2_, "B3": b3_, "B4": b4_,
                           "B5": b5_, "B6": b6_, "B7": b7_, **{f"B8_{j}": gelu(j) for j in range(4)},
                           "C1": c1_, "C2": c2_, "C3": c3_, "C4": c4_, **{f"C5_{g}": c_exp(g) for g in range(4)},
                           "C5_4": c5_4, "C6": c6_, "C6b": c6b_, "C7_0": c7(0), "C7_1": c7(1), "C8": c8_,
                           "C8b": c8b_},
                   (lambda: split_weights(0, LOADS_A), before_b,
                    lambda: split_weights(LOADS_A + LOADS_B, len(loads))))

        @block.vector
        def _(dve):
            ts, tt, stt = nc.vector.tensor_scalar, nc.vector.tensor_tensor, nc.vector.scalar_tensor_tensor

            def split_weights(lo, hi):
                for n in range(lo, hi):
                    dve.wait_ge(raw_hi.sem, n + 1)
                    tt(loads[n][2][1], raw[:, n % NRAW, 0:loads[n][1]], loads[n][2][0].bitcast(F32),
                       ALU.subtract).then_inc(raw_lo.sem, 1)

            def low(out_, full, high, done):
                tt(out_, full, high.bitcast(F32), ALU.subtract).then_inc(done.sem, 1)

            def statistics(b, src, st, mv, mean):
                for t in range(TT):
                    nc.vector.bn_stats(st[:, t, :], src[:, t, :]).then_inc(mean.sem, 1)
                for t in range(TT):
                    dve.wait_ge(*mean(b, t + 1))
                    dve.sem_inc(passed.sem, 1)
                    nc.vector.bn_aggr(mv[:, t, :], st[:, t, :]).then_inc(mean.sem, 1)

            def normalise(b, dst, src, mv, rs, rstd, normed):
                dve.wait_ge(*rstd(b))
                for t in range(TT):
                    ts(dst[:, t, :], src[:, t, :], mv[:, t, 0:1], rs[:, t:t + 1], ALU.subtract, ALU.mult) \
                        .then_inc(normed.sem, 1)

            def a1_(b):
                dve.wait_ge(*x_in(b))
                if not first(b):
                    dve.wait_ge(*a_done(b - 1))
                statistics(b, xin, a_st, a_mv, a_mean)
                normalise(b, a_norm, xin, a_mv, a_rs, a_rstd, a_normed)

            def a2_(b):
                dve.wait_ge(*a_thi(b))
                low(a_tr[1][:, :, :].rearrange("p c t -> p (c t)"), a0[:, :], a_tr[0][:, :, :]
                    .rearrange("p c t -> p (c t)"), a_tlo)

            def phi(out_, e, parts_done, done, b, k=None):
                dve.wait_ge(*parts_done(b, k))
                stt(out_, e, 1.0, out_, ALU.min, ALU.add).then_inc(done.sem, 1)

            def a3_(b):
                phi(qT[:, :, :].rearrange("p c t -> p (c t)"), a_e0[:, :], q_out, qk_phi, b)
                phi(kT[:, :, :].rearrange("p c t -> p (c t)"), a_e1[:, :], k_out, qk_phi, b)

            def a3b_(b):
                for t, bk in enumerate((a0, a1)):
                    phi(k_tok[:, t, :], a_s1[:, t * D:(t + 1) * D], kv_out, kv_phi, b, 2 * (t + 1))
                    for m in range(2):
                        nc.vector.tensor_copy(
                            vM[m][:, t, :].rearrange("p (n m e) -> p n m e", m=2, e=HD)[:, :, m, :],
                            bk[:, D:2 * D].rearrange("p (n m e) -> p n m e", m=2, e=HD)[:, :, m, :]) \
                            .then_inc(v_put.sem, 1)
                    if t == 0:
                        nc.vector.tensor_copy(v0[:, :], bk[:, D:2 * D]).then_inc(v_put.sem, 1)

            def a4_(b):
                dve.wait_ge(*s_mm(b))
                tt(state[:, :].rearrange("p (c e) -> p c e", c=DC), a2[:, 0:D].rearrange("p (c e) -> p c e", c=DC),
                   C["head_block"].unsqueeze(1).broadcast_to([P, DC, P]), ALU.mult).then_inc(s_put.sem, 1)
                dve.wait_ge(*ksum_mm(b))
                tt(a_e0[:, :], a0[:, :], qT[:, :, :].rearrange("p c t -> p (c t)"), ALU.mult).then_inc(ksum_q.sem, 1)

            def a4b_(b):
                dve.wait_ge(*den_mm(b))
                ts(a_e1[:, :], a0[:, :], DEN_EPS, None, ALU.add).then_inc(den_inv.sem, 1)
                dve.wait_ge(*den_inv(b, 1))
                nc.vector.reciprocal(a_e1[:, :], a_e1[:, :]).then_inc(den_inv.sem, 1)

            def a5(g):
                def step(b):
                    dve.wait_ge(*score_mm(b, g + 1))
                    if g >= 2:
                        dve.wait_ge(*av_mm(b, g - 1))
                    tt((a_s1, a_e0)[g % 2][:, :].rearrange("p (h q) -> p h q", h=4),
                       (a1, a2)[g % 2][:, :].rearrange("p (h q) -> p h q", h=4),
                       tri.unsqueeze(1).broadcast_to([P, 4, P]), ALU.mult).then_inc(score_put.sem, 1)
                return step

            def a5_8(b):
                dve.wait_ge(*av_mm(b))
                dve.wait_ge(*den_inv(b))
                tt(a_norm[:, :, :].rearrange("p c t -> p (c t)"), a0[:, :], a_e1[:, :], ALU.mult).then_inc(y_put.sem, 1)

            def a6_(b):
                dve.wait_ge(*y_hi(b))
                dve.wait_ge(*y_put(b))
                low(a_tr[1][:, :, :], a_norm[:, :, :], a_tr[0][:, :, :], y_lo)
                dve.wait_ge(*proj_mm(b))
                dve.wait_ge(*x_kept(b))
                tt(x1[:, :, :].rearrange("p t d -> p (t d)"), x1[:, :, :].rearrange("p t d -> p (t d)"), a1[:, :],
                   ALU.add).then_inc(a_done.sem, 1)

            def b1_(b):
                dve.wait_ge(*a_done(b))
                if not first(b):
                    dve.wait_ge(*b_done(b - 1))
                statistics(b, x1, b_st, b_mv, b_mean)
                normalise(b, qc, x1, b_mv, b_rs, b_rstd, q_normed)

            def b2_(b):
                dve.wait_ge(*p_exp(b))
                ts(prob[:, :, :], prob[:, :, :], 1.0, None, ALU.add).then_inc(p_inv.sem, 1)
                dve.wait_ge(*p_inv(b, 1))
                nc.vector.reciprocal(prob[:, :, :], prob[:, :, :]).then_inc(p_inv.sem, 1)
                dve.wait_ge(*p_raw(b))
                ts(b_rsum[:, :], b_sum[:, :], PROB_EPS, None, ALU.add).then_inc(p_rsum.sem, 1)
                dve.wait_ge(*p_rsum(b, 1))
                nc.vector.reciprocal(b_rsum[:, :], b_rsum[:, :]).then_inc(p_rsum.sem, 1)
                dve.wait_ge(*p_rsum(b))
                for s in range(2 * TT):
                    ts(prob[:, s, :], prob[:, s, :], b_rsum[:, s:s + 1], PROB_EPS, ALU.mult, ALU.max) \
                        .then_inc(p_norm.sem, 1)
                dve.wait_ge(*p_norm(b))
                tt(b_f0[:, :, :], prob[:, 0:TT, :], prob[:, TT:2 * TT, :], ALU.subtract).then_inc(diff_put.sem, 1)
                dve.wait_ge(*p_log(b))
                tt(b_f1[:, :, :], prob[:, 0:TT, :], prob[:, TT:2 * TT, :], ALU.subtract).then_inc(ratio_put.sem, 1)

            def b3_(b):
                dve.wait_ge(*dr_hi(b, 1))
                low(b_s0[1][:, :], b0[:, :], b_s0[0][:, :], dr_lo)
                dve.wait_ge(*dr_hi(b, 2))
                low(b_s1[1][:, :], b1[:, :], b_s1[0][:, :], dr_lo)

            def b4_(b):
                dve.wait_ge(*sid_mm(b))
                nc.vector.tensor_reduce(b_min[:, :], b0[:, :].rearrange("p (t m) -> p t m", t=TT), axis=AX.X,
                                        op=ALU.min).then_inc(sid_bias.sem, 1)
                dve.wait_ge(*sid_bias(b, 1))
                ts(b_bias[:, :], b_min[:, :], 1.0 / D ** 0.5, None, ALU.mult).then_inc(sid_bias.sem, 1)
                dve.wait_ge(*sid_exp(b))
                nc.vector.reciprocal(b_z[:, :], b_z[:, :]).then_inc(z_neg.sem, 1)
                dve.wait_ge(*z_neg(b, 1))
                ts(b_nz[:, :], b_z[:, :], -1.0, None, ALU.mult).then_inc(z_neg.sem, 1)
                dve.wait_ge(*z_neg(b))
                for t in range(TT):
                    stt(prob[:, TT + t, :], prob[:, t, :], b_nz[:, t:t + 1], ident2[:, t, :], ALU.mult, ALU.add) \
                        .then_inc(att_put.sem, 1)

            def b5_(b):
                dve.wait_ge(*att_hi(b))
                low(b_s0[1][:, :], b1[:, :], b_s0[0][:, :], att_lo)

            def b6_(b):
                dve.wait_ge(*fd_hi(b))
                low(b_s1[1][:, :], b0[:, :], b_s1[0][:, :], fd_lo)
                dve.wait_ge(*f_mm(b))
                dve.wait_ge(*qb_put(b))
                tt(b_f0[:, :, :].rearrange("p t d -> p (t d)"), b1[:, :], qb[:, :, :].rearrange("p t d -> p (t d)"),
                   ALU.add).then_inc(f_put.sem, 1)
                dve.wait_ge(*f_put(b))
                statistics(b, b_f0, b_st, b_mv, f_mean)

            def b7_(b):
                normalise(b, prob, b_f0, b_mv, b_rs, f_rstd, f_normed)
                dve.wait_ge(*h_tp(b))
                for c in range(DC):
                    ts(b_f1[:, c, :], b0[:, c * T:(c + 1) * T], ln_g_col[:, c:c + 1], ln_b_col[:, c:c + 1], ALU.mult,
                       ALU.add).then_inc(h_aff.sem, 1)
                dve.wait_ge(*h_hi(b))
                dve.wait_ge(*h_aff(b))
                low(b_s0[1][:, :], b_f1[:, :, :].rearrange("p c t -> p (c t)"), b_s0[0][:, :], h_lo)

            def b8(j):
                def step(b):
                    hi, lo = (b_s2, b_s1)[j % 2]
                    src = prob[:, 2 * (j % 2):2 * (j % 2) + 2, :].rearrange("p t d -> p (t d)")
                    dve.wait_ge(*gelu_put(b, 2 * j + 2))
                    if j >= 2:
                        dve.wait_ge(*down_mm(b, j - 1))
                    nc.vector.tensor_copy(hi[:, :], src).then_inc(g_hi.sem, 1)
                    dve.wait_ge(*g_hi(b, j + 1))
                    low(lo[:, :], src, hi[:, :], g_lo)
                return step

            def b9_(b):
                dve.wait_ge(*down_mm(b))
                dve.wait_ge(*f_kept(b))
                tt(b_f0[:, :, :].rearrange("p t d -> p (t d)"), b1[:, :], qb[:, :, :].rearrange("p t d -> p (t d)"),
                   ALU.add).then_inc(o_put.sem, 1)
                dve.wait_ge(*o_put(b))
                statistics(b, b_f0, b_st, b_mv, o_mean)

            def b9b_(b):
                normalise(b, b_f0, b_f0, b_mv, b_rs, o_rstd, o_normed)
                dve.wait_ge(*o_normed(b))
                tt(b_f0[:, :, :], b_f0[:, :, :], ln_g_bc.unsqueeze(1).broadcast_to([P, TT, D]), ALU.mult) \
                    .then_inc(o_gain.sem, 1)
                dve.wait_ge(*o_gain(b))
                dve.wait_ge(*x1_kept(b))
                tt(x2[:, :, :], x2[:, :, :], b_f0[:, :, :], ALU.add).then_inc(b_done.sem, 1)

            def c1_(b):
                dve.wait_ge(*b_done(b))
                if first(b):
                    dve.wait_ge(raw_lo.sem, len(loads))
                else:
                    dve.wait_ge(*c_done(b - 1))
                statistics(b, x2, c_st, c_mv, c_mean)
                normalise(b, c_norm, x2, c_mv, c_rs, c_rstd, c_normed)
                for t in range(TT):
                    dve.wait_ge(*c_normed(b, t + 1))
                    nc.vector.tensor_tensor_reduce(out=tie[:, :], in0=c_norm[:, t, :], in1=router_bc, scale=1.0,
                                                   scalar=0.0, op0=ALU.mult, op1=ALU.add,
                                                   accum_out=c_sc[:, t:t + 1]).then_inc(r_score.sem, 1)
                    dve.wait_ge(*r_score(b, t + 1))

            def c2_(b):
                dve.wait_ge(*sc_bc(b))
                for t in range(TT):
                    if t:
                        dve.wait_ge(*before_put(b, 2 * t))
                    stt(tie[:, :], c0[:, 0:T], c_sc[:, t:t + 1], tie_mask[:, t, :], ALU.is_equal, ALU.mult) \
                        .then_inc(before_put.sem, 1)
                    dve.wait_ge(*before_put(b, 2 * t + 1))
                    stt(before[:, t, :], c0[:, 0:T], c_sc[:, t:t + 1], tie[:, :], ALU.is_lt, ALU.add) \
                        .then_inc(before_put.sem, 1)
                dve.wait_ge(*rank_mm(b))
                ts(sel_t[:, :], c1[:, 0:T], C["iota"], None, ALU.is_equal).then_inc(selt_put.sem, 1)

            def c4_(b):
                dve.wait_ge(*hg_mm(b))
                for c in range(DC):
                    ts(c_hT[:, c, :], c0[:, c * R:(c + 1) * R], g1_col[:, c:c + 1], None, ALU.mult) \
                        .then_inc(hg_put.sem, 1)
                dve.wait_ge(*hg_hi(b))
                dve.wait_ge(*hg_put(b))
                low(c_hs[1][:, :, :], c_hT[:, :, :], c_hs[0][:, :, :], hg_lo)
                dve.wait_ge(*cv_mm(b))
                for m in range(2):
                    nc.vector.tensor_copy(cv[m][:, :].rearrange("p (n m e) -> p n m e", m=2, e=HD)[:, :, m, :],
                                          c0[:, 0:D].rearrange("p (n m e) -> p n m e", m=2, e=HD)[:, :, m, :]) \
                        .then_inc(cv_put.sem, 1)

            def c_mask(g):
                def step(b):
                    logits = (c_norm, c_pre)[g % 2][:, :, :].rearrange("p t d -> p (t d)") \
                        .rearrange("p (h k) -> p h k", h=4)
                    dve.wait_ge(*cs_mm(b, g + 1))
                    if g == 0:
                        dve.wait_ge(*ob_put(b))
                    if g >= 2:
                        dve.wait_ge(*cs_tp(b, g - 1))
                        dve.wait_ge(*cs_sum(b, g - 1))
                    tt(logits, (c1, c2)[g % 2][:, :].rearrange("p (h k) -> p h k", h=4),
                       neg_mask.unsqueeze(1).broadcast_to([P, 4, R]), ALU.add).then_inc(cs_max.sem, 1)
                    dve.wait_ge(*cs_max(b, 2 * g + 1))
                    nc.vector.tensor_reduce(c_max[:, 4 * g:4 * g + 4], logits, axis=AX.X, op=ALU.max) \
                        .then_inc(cs_max.sem, 1)
                    if g >= 1:
                        c_total(b, g - 1)
                return step

            def c_total(b, g):
                logits = (c_norm, c_pre)[g % 2][:, :, :].rearrange("p t d -> p (t d)") \
                    .rearrange("p (h k) -> p h k", h=4)
                dve.wait_ge(*cs_exp(b, g + 1))
                nc.vector.tensor_reduce(c_den[:, 4 * g:4 * g + 4], logits, axis=AX.X, op=ALU.add) \
                    .then_inc(cs_sum.sem, 1)

            def c5_4(b):
                c_total(b, 3)
                dve.wait_ge(*cs_sum(b))
                nc.vector.reciprocal(c_den[:, :], c_den[:, :]).then_inc(cden_bc.sem, 1)
                dve.wait_ge(*cden_bc(b, 1))
                for c in range(DC):
                    nc.vector.tensor_copy(
                        c_rden[:, c * P:(c + 1) * P].rearrange("p (g m e) -> p g m e", m=2, e=HD),
                        c_den[:, :].rearrange("p (g c m) -> p g c m", c=DC, m=2)[:, :, c, :].unsqueeze(3)
                        .broadcast_to([P, NH // 4, 2, HD])).then_inc(cden_bc.sem, 1)
                dve.wait_ge(*cden_put(b))
                dve.wait_ge(*cav_mm(b))
                tt(c_hT[:, :, :].rearrange("p c r -> p (c r)"), c0[:, 0:D], c_rT[:, :], ALU.mult).then_inc(co_put.sem, 1)

            def c6_(b):
                dve.wait_ge(*co_hi(b))
                dve.wait_ge(*co_put(b))
                low(c_hs[1][:, :, :], c_hT[:, :, :], c_hs[0][:, :, :], co_lo)
                dve.wait_ge(*xo_put(b))
                dve.wait_ge(*xs_put(b))
                tt(c_h2[:, :], c0[:, 0:D], x_sel[:, :], ALU.add).then_inc(h2_sum.sem, 1)
                dve.wait_ge(*h2_rms(b))
                ts(c_h2n[:, :], c_h2[:, :], c_rms2[:, :], None, ALU.mult).then_inc(h2_norm.sem, 1)

            def c6b_(b):
                dve.wait_ge(*h2_tp(b))
                for c in range(DC):
                    ts(c_hT[:, c, :], c1[:, c * R:(c + 1) * R], g2_col[:, c:c + 1], None, ALU.mult) \
                        .then_inc(h2_put.sem, 1)
                dve.wait_ge(*h2_hi(b))
                dve.wait_ge(*h2_put(b))
                low(c_hs[1][:, :, :], c_hT[:, :, :], c_hs[0][:, :, :], h2_lo)

            def c7(j):
                def step(b):
                    n = (FG, FF - FG)[j]
                    gate, val = c_et[0][:, 0:n], c_et[1][:, 0:n]
                    dve.wait_ge(*g_exp(b, j + 1))
                    ts(gate, gate, 1.0, None, ALU.add).then_inc(g_inv.sem, 1)
                    dve.wait_ge(*g_inv(b, 2 * j + 1))
                    nc.vector.reciprocal(gate, gate).then_inc(g_inv.sem, 1)
                    dve.wait_ge(*g_inv(b, 2 * j + 2))
                    dve.wait_ge(*gu_mm(b, j + 1))
                    if j:
                        dve.wait_ge(*g_act(b, 1))
                    tt(val, c1[:, 0:n], gate, ALU.mult).then_inc(g_gate.sem, 1)
                    dve.wait_ge(*g_gate(b, j + 1))
                    tt(act[:, j * FG:j * FG + n], c2[:, 0:n], val, ALU.mult).then_inc(g_act.sem, 1)
                return step

            def c8_(b):
                for j, (bk, s) in enumerate(((c1, slice(0, 4)), (c2, slice(4, 6)))):
                    n = (s.stop - s.start) * R
                    dve.wait_ge(*at_hi(b, j + 1))
                    low(act_t[1][:, s, :].rearrange("p c r -> p (c r)"), bk[:, 0:n],
                        act_t[0][:, s, :].rearrange("p c r -> p (c r)"), at_lo)
                dve.wait_ge(*ff_mm(b))
                dve.wait_ge(*xo_put(b))
                tt(c_h2[:, :], c0[:, D:2 * D], x_att[:, :], ALU.add).then_inc(ff_put.sem, 1)

            def c8b_(b):
                dve.wait_ge(*ff_hi(b))
                dve.wait_ge(*ff_put(b))
                low(c_hs[1][:, :, :].rearrange("p c r -> p (c r)"), c_h2[:, :], c_hs[0][:, :, :]
                    .rearrange("p c r -> p (c r)"), ff_lo)
                dve.wait_ge(*scat_mm(b))
                dve.wait_ge(*ob_put(b))
                tt(ob[:, :, :].rearrange("p t d -> p (t d)"), ob[:, :, :].rearrange("p t d -> p (t d)"), c1[:, :],
                   ALU.add).then_inc(c_done.sem, 1)

            for buf in (*vM, *cv):
                nc.vector.memset(buf[:], 0.0).then_inc(v_zero.sem, 1)
            nc.vector.memset(act[:, FF:FFP], 0.0).then_inc(v_zero.sem, 1)
            dve.wait_ge(v_zero.sem, 5)
            dve.wait_ge(const_in.sem, 16)

            def before_b():
                split_weights(LOADS_A, LOADS_A + LOADS_B)
                dve.wait_ge(vec_in.sem, 32)

            rounds(dve, {"A1": a1_, "A2": a2_, "A3": a3_, "A3b": a3b_, "A4": a4_, "A4b": a4b_,
                         **{f"A5_{g}": a5(g) for g in range(8)}, "A5_8": a5_8, "A6": a6_,
                         "B1": b1_, "B2": b2_, "B3": b3_, "B4": b4_, "B5": b5_, "B6": b6_, "B7": b7_,
                         **{f"B8_{j}": b8(j) for j in range(4)}, "B9": b9_, "B9b": b9b_,
                         "C1": c1_, "C2": c2_, "C4": c4_, **{f"C5_{g}": c_mask(g) for g in range(4)}, "C5_4": c5_4,
                         "C6": c6_, "C6b": c6b_, "C7_0": c7(0), "C7_1": c7(1), "C8": c8_, "C8b": c8b_},
                   (lambda: split_weights(0, LOADS_A), before_b,
                    lambda: split_weights(LOADS_A + LOADS_B, len(loads))))

        @block.tensor
        def _(pe):
            mm = nc.tensor.matmul
            PASSES = ((0, 0), (0, 1), (1, 0))
            GROUP = ((0, 0), (0, 1), (1, 0), (1, 1))

            def split_product(out_, lhs, rhs, n, start=True, stop=True, **kw):
                last = None
                for a, (p, q) in enumerate(PASSES):
                    for k in range(n):
                        last = mm(out_, lhs(p, k), rhs(q, k), start=start and a == 0 and k == 0,
                                  stop=stop and a == 2 and k == n - 1, **kw)
                return last

            def transposes(bank_, src, n_out, n_in, width=P):
                last = None
                for o in range(n_out):
                    for i in range(n_in):
                        at = (o * n_in + i) * P
                        last = nc.tensor.transpose(bank_[:, at:at + P], src[:, i, o * P:(o + 1) * P], ident)
                return last

            def a2_(b):
                pe.wait_ge(*a_normed(b))
                transposes(a0, a_norm, DC, TT).then_inc(a_tp.sem, 1)

            def a3_(b):
                pe.wait_ge(*a_thi(b))
                pe.wait_ge(*a_tlo(b))
                for which, bk in enumerate((a1, a2)):
                    for m in range(DC):
                        last = split_product(bk[:, m * T:(m + 1) * T],
                                             lambda p, k: wa[p][:, k, which * D + m * P:which * D + (m + 1) * P],
                                             lambda p, k: a_tr[p][:, k, :], DC)
                    last.then_inc(qk_mm.sem, 1)

            def a3b_(b):
                for t, bk in enumerate((a0, a1)):
                    if t == 1:
                        pe.wait_ge(*q_out(b))
                    split_product(bk[:, :], lambda p, k: a_tr[p][:, k, t * P:(t + 1) * P],
                                  lambda p, k: wa[p][:, k, D:3 * D], DC).then_inc(kv_mm.sem, 1)

            def a4_(b):
                pe.wait_ge(*kv_phi(b))
                pe.wait_ge(*v_put(b))
                for c in range(DC):
                    cs = slice(c * P, (c + 1) * P)
                    mm(a0[:, c * T:(c + 1) * T], k_tok[:, 0, cs], C["tri_ones"], start=True, stop=False)
                    last = mm(a0[:, c * T + P:(c + 1) * T], k_tok[:, 1, cs], tri, start=False, stop=True)
                last.then_inc(ksum_mm.sem, 1)
                pe.wait_ge(*qk_phi(b))
                for c in range(DC):
                    cs = slice(c * P, (c + 1) * P)
                    last = mm(a2[:, cs], k_tok[:, 0, cs], v0[:, cs], start=True, stop=True)
                last.then_inc(s_mm.sem, 1)

            def a4b_(b):
                pe.wait_ge(*ksum_q(b))
                mm(a0[:, :], C["head_block"], a_e0[:, :], start=True, stop=True).then_inc(den_mm.sem, 1)

            def scores(b, g):
                t, bk, r = g // 4, (a1, a2)[g % 2], 32 * (g % 4)
                for j, (c, m) in enumerate(GROUP):
                    last = mm(bk[:, j * P:(j + 1) * P], kT[r:r + 32, c, t * P:(t + 1) * P],
                              qM[m][r:r + 32, c, t * P:(t + 1) * P], start=True, stop=True)
                last.then_inc(score_mm.sem, 1)

            def attend(b, g):
                t, r = g // 4, 32 * (g % 4)
                pe.wait_ge(*score_put(b, g + 1))
                if g == 4:
                    for c in range(DC):
                        mm(a0[:, c * T + P:(c + 1) * T], state[:, c * P:(c + 1) * P], qT[:, c, P:2 * P],
                           start=c == 0, stop=False, skip_group_check=True)
                for j, (c, m) in enumerate(GROUP):
                    last = mm(a0[r:r + 32, c * T + t * P:c * T + (t + 1) * P],
                              vM[m][:, t, c * P + r:c * P + r + 32],
                              (a_s1, a_e0)[g % 2][:, j * P:(j + 1) * P], start=t == 0 and m == 0,
                              stop=m == 1, skip_group_check=True)
                last.then_inc(av_mm.sem, 1)

            def a5(g):
                def step(b):
                    if g == 0:
                        pe.wait_ge(*q_mask(b))
                        pe.wait_ge(*s_put(b))
                        pe.wait_ge(*v_put(b))
                    if g >= 2:
                        pe.wait_ge(*score_put(b, g - 1))
                    if g < 8:
                        scores(b, g)
                    if g == 1:
                        pe.wait_ge(*den_inv(b, 1))
                    if g >= 1:
                        attend(b, g - 1)
                return step

            def a6_(b):
                pe.wait_ge(*y_hi(b))
                pe.wait_ge(*y_lo(b))
                for t in range(TT):
                    last = split_product(a1[:, t * D:(t + 1) * D], lambda p, k: a_tr[p][:, k, t * P:(t + 1) * P],
                                         lambda p, k: wp[p][:, k, :], DC)
                last.then_inc(proj_mm.sem, 1)

            def b3_(b):
                pe.wait_ge(*diff_put(b))
                transposes(b0, b_f0, DC, TT).then_inc(dr_tp.sem, 1)
                pe.wait_ge(*ratio_put(b))
                transposes(b1, b_f1, DC, TT).then_inc(dr_tp.sem, 1)

            def b3b_(b):
                for s in (dr_hi, dr_lo):
                    pe.wait_ge(*s(b))
                for t in range(TT):
                    last = split_product(b0[:, t * T:(t + 1) * T],
                                         lambda p, k: b_s0[p][:, k * T + t * P:k * T + (t + 1) * P],
                                         lambda p, k: b_s1[p][:, k * T:(k + 1) * T], DC)
                last.then_inc(sid_mm.sem, 1)

            def b5_(b):
                pe.wait_ge(*att_put(b))
                transposes(b1, prob[:, TT:2 * TT, :], TT, TT).then_inc(att_tp.sem, 1)

            def b6_(b):
                for s in (att_hi, att_lo, c_hi, c_lo):
                    pe.wait_ge(*s(b))
                for c in range(DC):
                    last = split_product(b0[:, c * T:(c + 1) * T],
                                         lambda p, k: b_s2[p][:, k * D + c * P:k * D + (c + 1) * P],
                                         lambda p, k: b_s0[p][:, k * T:(k + 1) * T], TT)
                last.then_inc(fd_mm.sem, 1)
                pe.wait_ge(*fd_hi(b))
                pe.wait_ge(*fd_lo(b))
                for t in range(TT):
                    last = split_product(b1[:, t * D:(t + 1) * D],
                                         lambda p, k: b_s1[p][:, k * T + t * P:k * T + (t + 1) * P],
                                         lambda p, k: wd[p][:, k, :], DC)
                last.then_inc(f_mm.sem, 1)

            def b7_(b):
                pe.wait_ge(*f_normed(b))
                transposes(b0, prob, DC, TT).then_inc(h_tp.sem, 1)

            def mlp_down(b, j):
                part = (b_s2, b_s1)[j % 2]
                pe.wait_ge(*g_hi(b, j + 1))
                pe.wait_ge(*g_lo(b, j + 1))
                for t in range(TT):
                    for a, (p, q) in enumerate(PASSES):
                        for n in range(2):
                            last = mm(b1[:, t * D:(t + 1) * D], part[p][:, n * T + t * P:n * T + (t + 1) * P],
                                      w2[q][:, 2 * j + n, :], start=j == 0 and t == 0 and a == 0 and n == 0,
                                      stop=j == 3 and a == 2 and n == 1, skip_group_check=True)
                last.then_inc(down_mm.sem, 1)

            def b8(j):
                def step(b):
                    if j == 0:
                        pe.wait_ge(*h_hi(b))
                        pe.wait_ge(*h_lo(b))
                        pe.wait_ge(*f_put(b))
                    else:
                        pe.wait_ge(*gelu_put(b, 2 * j))
                    for n in range(2):
                        f = 2 * j + n
                        last = split_product(b0[:, n * T:(n + 1) * T], lambda p, k: w1[p][:, k, f * P:(f + 1) * P],
                                             lambda p, k: b_s0[p][:, k * T:(k + 1) * T], DC)
                    last.then_inc(up_mm.sem, 1)
                    if j >= 1:
                        mlp_down(b, j - 1)
                return step

            def b9_(b):
                mlp_down(b, 3)

            def c2_(b):
                pe.wait_ge(*r_score(b))
                for t in range(TT):
                    last = nc.tensor.transpose(c0[:, t * P:(t + 1) * P], c_sc[:, t:t + 1].broadcast_to([P, P]), ident)
                last.then_inc(sc_bc.sem, 1)
                pe.wait_ge(*before_put(b))
                for t in range(TT):
                    last = mm(c1[:, 0:T], ones_bf[:, :], before[:, t, :], start=t == 0, stop=t == TT - 1)
                last.then_inc(rank_mm.sem, 1)

            def c3_(b):
                pe.wait_ge(*selt_put(b))
                for t in range(TT):
                    last = nc.tensor.transpose(c2[:, t * R:(t + 1) * R], sel_t[:, t * P:(t + 1) * P].bitcast(F32),
                                               ident)
                last.then_inc(sel_tp.sem, 1)
                pe.wait_ge(*sel_put(b))
                pe.wait_ge(*pre_put(b))
                for c in range(DC):
                    for t in range(TT):
                        last = mm(c0[:, c * R:(c + 1) * R], c_pre[:, t, c * P:(c + 1) * P], sel[:, t, :],
                                  start=t == 0, stop=t == TT - 1)
                last.then_inc(hg_mm.sem, 1)
                for t in range(TT):
                    last = mm(c1[:, 0:D], sel[:, t, :], c_norm[:, t, :], start=t == 0, stop=t == TT - 1)
                last.then_inc(xs_mm.sem, 1)

            def c4_(b):
                pe.wait_ge(*hg_put(b))
                for m in range(2 * DC):
                    for k in range(DC):
                        last = mm(c2[:, m * R:(m + 1) * R], wcqk[:, k, m * P:(m + 1) * P], c_hT[:, k, :],
                                  start=k == 0, stop=k == DC - 1)
                last.then_inc(cqk_mm.sem, 1)
                pe.wait_ge(*hg_hi(b))
                pe.wait_ge(*hg_lo(b))
                split_product(c0[:, 0:D], lambda p, k: c_hs[p][:, k, :], lambda p, k: wcv[p][:, k, :], DC) \
                    .then_inc(cv_mm.sem, 1)

            def c_scores(b, g):
                r = 32 * g
                for j, (c, m) in enumerate(GROUP):
                    last = mm((c1, c2)[g % 2][:, j * R:(j + 1) * R], cq[m][r:r + 32, c, :], ck[r:r + 32, c, :],
                              start=True, stop=True)
                last.then_inc(cs_mm.sem, 1)

            def c_turn(b, g):
                logits = (c_norm, c_pre)[g % 2][:, :, :].rearrange("p t d -> p (t d)")
                pe.wait_ge(*cs_exp(b, g + 1))
                for j in range(4):
                    last = nc.tensor.transpose((c1, c2)[g % 2][:, j * R:(j + 1) * R], logits[:, j * R:(j + 1) * R],
                                               ident)
                last.then_inc(cs_tp.sem, 1)

            def c_attend(b, g):
                pe.wait_ge(*cs_et(b, g + 1))
                r = 32 * g
                for j, (c, m) in enumerate(GROUP):
                    last = mm(c0[r:r + 32, c * R:(c + 1) * R], cv[m][:, c * P + r:c * P + r + 32],
                              c_et[g % 2][:, j * R:(j + 1) * R], start=m == 0, stop=m == 1,
                              skip_group_check=True)
                last.then_inc(cav_mm.sem, 1)

            def c5(g):
                def step(b):
                    if g == 0:
                        pe.wait_ge(*cqk_put(b))
                        pe.wait_ge(*xs_put(b))
                    if g >= 2:
                        pe.wait_ge(*cs_et(b, g - 1))
                    if g < 4:
                        c_scores(b, g)
                    if g == 1:
                        pe.wait_ge(*cv_put(b))
                    if g >= 1:
                        c_turn(b, g - 1)
                        if g >= 2:
                            c_attend(b, g - 2)
                return step

            def c5_4(b):
                c_turn(b, 3)
                c_attend(b, 2)
                c_attend(b, 3)
                pe.wait_ge(*cden_bc(b))
                for c in range(DC):
                    last = nc.tensor.transpose(c0[:, D + c * R:D + (c + 1) * R], c_rden[:, c * P:(c + 1) * P], ident)
                last.then_inc(cden_tp.sem, 1)

            def c6_(b):
                pe.wait_ge(*co_hi(b))
                pe.wait_ge(*co_lo(b))
                split_product(c0[:, 0:D], lambda p, k: c_hs[p][:, k, :], lambda p, k: wo[p][:, k, :], DC) \
                    .then_inc(xo_mm.sem, 1)

            def c6b_(b):
                pe.wait_ge(*h2_norm(b))
                for c in range(DC):
                    last = nc.tensor.transpose(c1[:, c * R:(c + 1) * R], c_h2n[:, c * P:(c + 1) * P], ident)
                last.then_inc(h2_tp.sem, 1)

            def c7(j):
                def step(b):
                    n = (FG, FF - FG)[j]
                    pe.wait_ge(*h2_hi(b))
                    pe.wait_ge(*h2_lo(b))
                    if j:
                        pe.wait_ge(*g_act(b, 1))
                    for which, bk in enumerate((c1, c2)):
                        last = split_product(bk[:, 0:n], lambda p, k: c_hs[p][:, k, :],
                                             lambda p, k: wgu[p][:, k, which * FF + j * FG:which * FF + j * FG + n],
                                             DC)
                    last.then_inc(gu_mm.sem, 1)
                return step

            def c8_(b):
                pe.wait_ge(*g_act(b))
                for j, (bk, lo, hi) in enumerate(((c1, 0, 4), (c2, 4, 6))):
                    for f in range(lo, hi):
                        last = nc.tensor.transpose(bk[:, (f - lo) * R:(f - lo + 1) * R], act[:, f * P:(f + 1) * P],
                                                   ident)
                    last.then_inc(at_tp.sem, 1)
                pe.wait_ge(*at_hi(b))
                pe.wait_ge(*at_lo(b))
                split_product(c0[:, D:2 * D], lambda p, k: act_t[p][:, k, :], lambda p, k: w3[p][:, k, :], FFP // P) \
                    .then_inc(ff_mm.sem, 1)

            def c8b_(b):
                pe.wait_ge(*ff_hi(b))
                pe.wait_ge(*ff_lo(b))
                for t in range(TT):
                    for p in range(2):
                        last = mm(c1[:, t * D:(t + 1) * D], sel_t[:, t * P:(t + 1) * P],
                                  c_hs[p][:, :, :].rearrange("p c r -> p (c r)"), start=p == 0, stop=p == 1)
                last.then_inc(scat_mm.sem, 1)

            pe.wait_ge(const_in.sem, 16)
            pe.wait_ge(ones_set.sem, 1)
            pe.wait_ge(v_zero.sem, 5)

            def weights_to(n):
                def step():
                    pe.wait_ge(raw_hi.sem, n)
                    pe.wait_ge(raw_lo.sem, n)
                    if n == len(loads):
                        pe.wait_ge(qk_in.sem, 16)
                return step

            rounds(pe, {"A2": a2_, "A3": a3_, "A3b": a3b_, "A4": a4_, "A4b": a4b_, **{f"A5_{g}": a5(g) for g in range(9)},
                        "A6": a6_, "B3": b3_, "B3b": b3b_, "B5": b5_, "B6": b6_, "B7": b7_,
                        **{f"B8_{j}": b8(j) for j in range(4)}, "B9": b9_,
                        "C2": c2_, "C3": c3_, "C4": c4_, **{f"C5_{g}": c5(g) for g in range(4)}, "C5_4": c5_4,
                        "C6": c6_, "C6b": c6b_, "C7_0": c7(0), "C7_1": c7(1), "C8": c8_, "C8b": c8b_},
                   (weights_to(LOADS_A), weights_to(LOADS_A + LOADS_B), weights_to(len(loads))))


def constants():
    p = np.arange(P)
    t = np.arange(T)
    c = np.zeros((P, NCONST), np.float32)
    c[:, CONST["ident2"]] = np.stack([t[None] == n * P + p[:, None] for n in range(TT)], 1).reshape(P, -1)
    c[:, CONST["tri_ones"]] = p[:, None] <= t[None]
    c[:, CONST["neg_mask"]] = np.where(p[None] > p[:, None], NEG, 0.0)
    c[:, CONST["head_block"]] = p[:, None] // HD == p[None] // HD
    c[:, CONST["tie_mask"]] = np.stack([n * P + p[:, None] < t[None] for n in range(TT)], 1).reshape(P, -1)
    c[:, CONST["iota"]] = p[:, None]
    even = (p // HD % 2 == 0).astype(np.float32)[:, None]
    c[:, CONST["even"]], c[:, CONST["odd"]] = even, 1 - even
    c[:, CONST["even4"]], c[:, CONST["odd4"]] = even / HD ** 0.5, (1 - even) / HD ** 0.5
    c[:, CONST["minus_half"]] = -0.5
    c[:, CONST["prob_bias"]] = 0.999
    return c


def kernel(**inputs):
    import concourse.bacc as bacc
    from concourse.bass_utils import run_bass_kernel_spmd

    a = {k: np.asarray(v) for k, v in inputs.items()}

    def by_input(w, n_in):
        return np.ascontiguousarray(w.T.reshape(n_in, P, w.shape[0]).transpose(1, 0, 2))

    def column(v):
        return v.reshape(-1, P).T

    w3 = np.zeros((D, FFP), np.float32)
    w3[:, :FF] = a["L0_ffn_W3"]
    gu = np.concatenate([a["L0_ffn_W1"], a["L0_ffn_W2"]], 0)
    by_row = [a[f"L0_{n}"] for n in ("xattn_ln_g", "xattn_ln_b", "xattn_b2", "xattn_b_diff", "ffn_w_router")]
    by_col = [a[f"L0_{n}"] for n in ("xattn_ln_g", "xattn_ln_b", "ffn_g1", "ffn_g2", "xattn_b1")]
    arrays = {
        "x": a["x"].reshape(B * T, D),
        "ctx": a["ctx_1024"].reshape(B * T, D),
        "consts": constants(),
        "vec_bc": np.ascontiguousarray(np.broadcast_to(np.stack(by_row)[None], (P, 5, D))),
        "vec_cols": np.ascontiguousarray(np.concatenate([column(v) for v in by_col], 1)),
        "w_a": by_input(a["L0_attn_w_attn"], DC),
        "w_proj": by_input(a["L0_attn_w_proj"], DC).reshape(P, -1),
        "w_diff": by_input(a["L0_xattn_W_diff"], DC).reshape(P, -1),
        "w_1": by_input(a["L0_xattn_W1"], DC),
        "w_2": by_input(a["L0_xattn_W2"], MLP // P),
        "w_cqk": by_input(a["L0_ffn_W_qkv"][:2 * D], DC),
        "w_cv": by_input(a["L0_ffn_W_qkv"][2 * D:], DC).reshape(P, -1),
        "w_out": by_input(a["L0_ffn_W_out"], DC).reshape(P, -1),
        "w_gu": by_input(gu, DC),
        "w_3": by_input(w3, FFP // P),
    }
    nc = bacc.Bacc("TRN2", target_bir_lowering=False, num_devices=1)
    args = [nc.dram_tensor(f"in_{k}", v.shape, F32, kind="ExternalInput").ap() for k, v in arrays.items()]
    out = nc.dram_tensor("out_0", (B * T, D), F32, kind="ExternalOutput").ap()
    decoder(nc, *args, out)
    r = run_bass_kernel_spmd(nc, [{f"in_{k}": v for k, v in arrays.items()}], core_ids=[0])
    return r.results[0]["out_0"].reshape(B, T, D)
```

```python
from contextlib import ExitStack

import numpy as np

import concourse.bass as bass
from concourse import mybir

F32 = mybir.dt.float32
F32R = mybir.dt.float32r
BF16 = mybir.dt.bfloat16
ALU = mybir.AluOpType
ACT = mybir.ActivationFunctionType
AX = mybir.AxisListType

B, T, D = 16, 256, 256
P = 128
TT = T // P
DC = D // P
NH, HD = 16, 16
R = 128
MLP = 1024
FF = 682
FFP = 768
FG = 342
LN_EPS, RMS_EPS, DEN_EPS, PROB_EPS = 1e-5, 1e-6, 1e-6, 1e-8
NEG = -3.0e38
NRAW = 3
ROW = D * TT

CONST = {}
_at = 0
for _name, _n in (("ident2", TT * T), ("tri_ones", T), ("neg_mask", P), ("head_block", P),
                  ("tie_mask", TT * T), ("iota", 1), ("even", 1), ("odd", 1), 
                  ("minus_half", TT), ("prob_bias", 1), ("chunk_heads", NH // DC)):
    CONST[_name] = slice(_at, _at + _n)
    _at += _n
NCONST = _at

ORDER = """
a_mean b_glo_2+ b_down_1+ b_ghi_3+ a_rstd a_ylo+ b_glo_3+ c_gu_0+ b_fb2+ c_tanh_0+ b_down_2+ c_gate_0+
a_normed b_down_3+ b_o+ b_omean+ c_gu_1+ c_tanh_1+ b_orstd+ c_gate_1+ c_gtp_0+ b_onormed+ c_gthi_0+ a_proj+
b_done+ a_tp c_gtp_1+ c_gtlo_0+ c_gthi_1+ a_done+ a_thi b_mean c_gtlo_1+ b_rstd c_mean b_normed c_rstd c_ff+
b_tanh c_normed b_qb c_rscore a_tlo c_y+ b_praw c_sbc c_yhi+ c_nhi b_chi b_pnorm c_ylo+ c_nlo b_diff a_kv_0
c_ob b_log c_before a_q c_scat+ c_done+ a_qout a_k b_ratio b_dtp c_rank b_rtp b_dhi c_selt c_seltp b_rhi
a_phi_q c_sel b_dlo a_kv_1 b_rlo a_kvout_0 c_xs a_kphi_0 a_kvout_1 a_kphi_1 b_sid c_xput c_rms b_sbias
a_kout a_ksum c_h a_state c_htp a_kq b_sexp a_den c_hput a_phi_k a_sput a_mask c_hhi a_dinv c_qk b_attn
a_score_0 c_qkput b_atp a_rden b_ahi a_score_1 b_clo b_alo c_score_0 a_scput_0 c_hlo b_fd a_rtp c_smask_0
b_fdhi c_v b_fdlo c_score_1 c_exp_0 c_vput a_dput b_f c_smask_1 c_etp_0 b_fput a_score_2 b_fmean c_exp_1
a_att_0 a_scput_1 c_etput_0 c_etp_1 b_frstd a_scput_2 c_etput_1 c_score_2 b_fnormed b_kept c_score_3 a_att_1
c_smask_2 a_score_3 a_kept c_att_0 c_smask_3 a_att_2 c_exp_2 b_htp a_scput_3 a_score_4 b_haff c_etp_2
c_att_1 a_att_3 c_exp_3 a_scput_4 b_hhi c_dinv a_score_5 c_etput_2 c_etp_3 a_scput_5 c_etput_3 b_hlo a_att_4
b_up_0 c_dtp b_gelu_0 a_score_6 c_att_2 c_att_3 a_att_5 c_dput a_scput_6 c_o b_ghi_0 b_up_1 c_ohi c_olo
a_score_7 b_gelu_1 b_glo_0 c_xo a_scput_7 c_h2s c_xoput c_h2sq b_ghi_1 b_up_2 a_att_6 a_att_7 b_gelu_2 a_y
c_h2rms c_h2n b_glo_1 b_down_0 a_yhi c_h2tp c_h2put c_h2hi c_h2lo b_ghi_2 b_up_3 b_gelu_3
""".split()
SKEW = {"a": 0, "b": 1, "c": 2}
STEPS = [(name.rstrip("+"), SKEW[name[0]] + name.count("+")) for name in ORDER]
FIRST = STEPS[0][0]
WEIGHTS_AT = {(0, FIRST): 3} | {(0, f"a_scput_{g}"): 1 for g in range(1, 8)} | {(1, FIRST): 1, (1, "b_pnorm"): 1,
              (1, "b_sbias"): 1, (1, "b_haff"): 2, (1, "b_o"): 1}
FILL = 1 + max(skew for _, skew in STEPS)


class Signal:

    def __init__(self, sem, per_row):
        self.sem, self.per_row = sem, per_row

    def __call__(self, b, k=None):
        return self.sem, b * self.per_row + (self.per_row if k is None else k)


def first(b):
    return isinstance(b, int) and b == 0


def rounds(eng, steps, weights=None):
    def one(i, outside=True):
        for name, skew in STEPS:
            if weights and outside and (i, name) in WEIGHTS_AT:
                weights(WEIGHTS_AT[i, name])
            if name in steps and not (outside and not 0 <= i - skew < B):
                steps[name](i - skew)

    for i in range(FILL):
        one(i)
    with eng.bass.Fori(FILL, B, engines=(eng.engine,), hint_back_edge=True) as i:
        one(i, outside=False)
    for i in range(B, B + FILL - 1):
        one(i)


def decoder(nc, x, ctx_in, consts, vec_bc, vec_cols, w_a, w_proj, w_diff, w_1, w_2, w_cqk, w_cv, w_out, w_gu, w_3, out):
    ctx = ExitStack()
    with ctx:
        def sb(name, shape, dt=F32):
            return ctx.enter_context(nc.sbuf_tensor(name, shape, dt))

        def sig(name, per_row=1):
            return Signal(ctx.enter_context(nc.semaphore(name)), per_row)

        const = sb("const", [P, NCONST])
        C = {n: const[:, s] for n, s in CONST.items()}
        tri, neg_mask = C["tri_ones"][:, 0:P], C["neg_mask"]
        ident2 = C["ident2"].rearrange("p (t n) -> p t n", t=TT)
        ident = ident2[:, 0, 0:P]
        tie_mask = C["tie_mask"].rearrange("p (t n) -> p t n", t=TT)
        ones_bf = sb("ones_bf", [P, P], BF16)
        bc = sb("vectors_by_row", [P, 5, D])
        ln_g_bc, ln_b_bc, b2_bc, b_diff_bc, router_bc = (bc[:, n, :] for n in range(5))
        cols = sb("vectors_by_column", [P, 4 * DC + MLP // P])
        ln_g_col, ln_b_col, g1_col, g2_col = (cols[:, n * DC:(n + 1) * DC] for n in range(4))
        b1_col = cols[:, 4 * DC:]

        def pair(name, shape):
            return sb(name + "_hi", shape, F32R), sb(name + "_lo", shape, F32R)

        wa = pair("w_attn", [P, DC, 3 * D])
        wp = pair("w_proj", [P, DC, D])
        wd = pair("w_diff", [P, DC, D])
        w1 = pair("w_mlp1", [P, DC, MLP])
        w2 = pair("w_mlp2", [P, MLP // P, D])
        wcv = pair("w_ffn_v", [P, DC, D])
        wo = pair("w_ffn_out", [P, DC, D])
        wgu = pair("w_ffn_gu", [P, DC, 2 * FF])
        w3 = pair("w_ffn_3", [P, FFP // P, D])
        wcqk = sb("w_ffn_qk", [P, DC, 2 * D])

        xin = sb("x_in", [P, TT, D])
        a_norm = sb("a_norm", [P, TT, D])
        a_tr = pair("a_tr", [P, DC, T])
        a_e0 = sb("a_e0", [P, 512])
        a_e1 = sb("a_e1", [P, 512])
        a_s1 = sb("a_s1", [P, 512])
        qT = sb("qT", [P, DC, T])
        qM = sb("qT_by_parity", [P, DC, TT, 2, P])
        kT = sb("kT", [P, DC, T])
        k_tok = sb("k_tok", [P, TT, D])
        vM = [sb("v_even", [P, TT, D]), sb("v_odd", [P, TT, D])]
        v0 = sb("v_first", [P, D])
        state = sb("state", [P, D])
        x1 = sb("x1", [P, TT, D])
        a_st = sb("a_st", [P, TT, 6])
        a_mv = sb("a_mv", [P, TT, 2])
        a_rs = sb("a_rs", [P, TT])
        a_r = sb("a_r", [P, TT * NH])

        qc = sb("qc", [P, 2 * TT, D])
        prob = sb("prob", [P, 2 * TT, D])
        b_f0 = sb("b_f0", [P, TT, D])
        b_f1 = sb("b_f1", [P, TT, D])
        b_s0 = pair("b_s0", [P, 512])
        b_s1 = pair("b_s1", [P, 512])
        b_s2 = pair("b_s2", [P, 512])
        qb = sb("q_bias", [P, TT, D])
        x2 = sb("x2", [P, TT, D])
        b_st = sb("b_st", [P, TT, 6])
        b_mv = sb("b_mv", [P, TT, 2])
        b_rs = sb("b_rs", [P, TT])
        f_st = sb("f_st", [P, TT, 6])
        f_mv = sb("f_mv", [P, TT, 2])
        f_rs = sb("f_rs", [P, TT])
        b_sum = sb("b_sum", [P, 2 * TT])
        b_rsum = sb("b_rsum", [P, 2 * TT])
        b_min = sb("b_min", [P, TT])
        b_bias = sb("b_bias", [P, TT])
        b_z = sb("b_z", [P, TT])

        raw = sb("w_raw_or_stage_c", [P, NRAW, MLP])
        parts = [raw[:, n // 2, n % 2 * ROW:(n % 2 + 1) * ROW] for n in range(5)]
        c_norm = parts[0].rearrange("p (t d) -> p t d", t=TT)
        c_odd = parts[1].rearrange("p (t d) -> p t d", t=TT)
        ob = parts[2].rearrange("p (t d) -> p t d", t=TT)
        c_et = parts[3:5]
        before = sb("before", [P, TT, T], BF16)
        tie = sb("tie", [P, T])
        sel_t = sb("select_by_rank", [P, T], F32R)
        sel = sb("select_by_token", [P, TT, R], F32R)
        c_hT = sb("c_hT", [P, DC, R])
        c_hs = pair("c_hs", [P, DC, R])
        x_sel = sb("x_sel", [P, D])
        cq = sb("c_q", [P, DC, R])
        ck = sb("c_k_by_parity", [P, DC, 2, R])
        cv = [sb("c_v_even", [P, D]), sb("c_v_odd", [P, D])]
        c_nmax = sb("c_nmax", [P, NH])
        c_den = sb("c_den", [P, NH])
        x_att = sb("x_att", [P, D])
        c_rT = x_att
        c_h2 = sb("c_h2", [P, D])
        c_h2n = sb("c_h2n", [P, D])
        c_rden = c_h2n
        act = sb("gated", [P, FFP])
        act_t = pair("gated_t", [P, FFP // P, R])
        c_st = sb("c_st", [P, TT, 6])
        c_mv = sb("c_mv", [P, TT, 2])
        c_rs = sb("c_rs", [P, TT])
        c_sc = sb("c_sc", [P, TT])
        c_sq = sb("c_sq", [P, 1])
        c_rms = sb("c_rms", [P, 1])
        c_sq2 = sb("c_sq2", [P, 1])
        c_rms2 = sb("c_rms2", [P, 1])


        bank = [ctx.enter_context(nc.psum_tensor(f"bank{n}", [P, 512], F32)) for n in range(8)]
        a0, a1, a2, b0, b1, c0, c1, c2 = bank

        loads = [
            *[(w_a[:, k, :], 3 * D, (wa[0][:, k, :], wa[1][:, k, :])) for k in range(DC)],
            (w_proj, DC * D, tuple(w[:, :, :].rearrange("p k n -> p (k n)") for w in wp)),
            (w_diff, DC * D, tuple(w[:, :, :].rearrange("p k n -> p (k n)") for w in wd)),
            *[(w_1[:, k, :], MLP, (w1[0][:, k, :], w1[1][:, k, :])) for k in range(DC)],
            *[(w_2[:, 4 * k:4 * k + 4, :].rearrange("p k n -> p (k n)"), 4 * D,
               tuple(w[:, 4 * k:4 * k + 4, :].rearrange("p k n -> p (k n)") for w in w2)) for k in range(2)],
            (w_cv, DC * D, tuple(w[:, :, :].rearrange("p k n -> p (k n)") for w in wcv)),
            (w_out, DC * D, tuple(w[:, :, :].rearrange("p k n -> p (k n)") for w in wo)),
            *[(w_gu[:, k, h * FF:(h + 1) * FF], FF, tuple(w[:, k, h * FF:(h + 1) * FF] for w in wgu))
              for k in range(DC) for h in range(2)],
            *[(w_3[:, 3 * k:3 * k + 3, :].rearrange("p k n -> p (k n)"), 3 * D,
               tuple(w[:, 3 * k:3 * k + 3, :].rearrange("p k n -> p (k n)") for w in w3)) for k in range(2)],
        ]
        LOADS_A, LOADS_B = 3, 5

        const_in, vec_in, qk_in = sig("const_in"), sig("vec_in"), sig("qk_in")
        raw_in = [sig(f"raw_in{n}") for n in range(NRAW)]
        raw_hi, raw_lo, ones_set, v_zero = sig("raw_hi"), sig("raw_lo"), sig("ones_set"), sig("v_zero")
        x_in, ctx_in_s, out_done = sig("x_loaded", 16), sig("ctx_loaded", 16), sig("out_stored", 16)
        a_mean, a_rstd, a_normed, a_kept = sig("a_mean", 2 * TT), sig("a_rstd", 2), sig("a_normed", TT), sig("a_kept")
        a_tp, a_thi, a_tlo, a_qk, a_qout, a_kout, a_phi, a_mask = (
            sig("a_tp"), sig("a_thi"), sig("a_tlo"), sig("a_qk", 2), sig("a_qout", 2), sig("a_kout", 2),
            sig("a_phi", 2), sig("a_mask", 2))
        a_kv, a_kvout, a_kphi, a_v, a_state, a_sput, a_ksum, a_kq, a_den, a_dinv, a_rden, a_rtp, a_dput = (
            sig("a_kv", TT), sig("a_kvout", 2 * TT), sig("a_kphi", TT), sig("a_v", 2 * TT + 1), sig("a_state"),
            sig("a_sput"), sig("a_ksum"), sig("a_kq"), sig("a_den"), sig("a_dinv", 2), sig("a_rden"), sig("a_rtp"), sig("a_dput"))
        a_score, a_scput, a_att, a_y, a_yhi, a_ylo, a_proj, a_done = (
            sig("a_score", 8), sig("a_scput", 8), sig("a_att", 8), sig("a_y"), sig("a_yhi"), sig("a_ylo"),
            sig("a_proj"), sig("a_done"))
        b_mean, b_rstd, b_normed, b_kept, b_qb = (sig("b_mean", 2 * TT), sig("b_rstd", 2), sig("b_normed", TT),
                                                  sig("b_kept"), sig("b_qb"))
        b_chi, b_clo, b_tanh, b_praw, b_rsum_s, b_pnorm, b_diff, b_log, b_ratio = (
            sig("b_chi"), sig("b_clo"), sig("b_tanh"), sig("b_praw", 4), sig("b_rsum", 2), sig("b_pnorm", 4),
            sig("b_diff"), sig("b_log"), sig("b_ratio"))
        b_pairtp, b_pairhi, b_pairlo = sig("b_pairtp", 2), sig("b_pairhi", 2), sig("b_pairlo", 2)
        b_sid, b_sbias, b_sexp, b_zinv, b_attn, b_atp, b_ahi, b_alo = (
            sig("b_sid"), sig("b_sbias", 2), sig("b_sexp", TT), sig("b_zinv"), sig("b_attn", TT), sig("b_atp"),
            sig("b_ahi"), sig("b_alo"))
        b_fd, b_fdhi, b_fdlo, b_f, b_fput = (sig(f"b_{n}") for n in ("fd", "fdhi", "fdlo", "f", "fput"))
        b_fmean, b_frstd, b_fnormed, b_fb2, b_htp, b_haff, b_hhi, b_hlo = (
            sig("b_fmean", 2 * TT), sig("b_frstd", 2), sig("b_fnormed", TT), sig("b_fb2"), sig("b_htp"),
            sig("b_haff", DC), sig("b_hhi"), sig("b_hlo"))
        b_up, b_gelu, b_ghi, b_glo, b_down = sig("b_up", 4), sig("b_gelu", 8), sig("b_ghi", 4), sig("b_glo", 4), sig("b_down", 4)
        b_o, b_omean, b_orstd, b_onormed, b_ogain, b_done = (
            sig("b_o"), sig("b_omean", 2 * TT), sig("b_orstd", 2), sig("b_onormed", TT), sig("b_ogain"), sig("b_done"))
        c_mean, c_rstd, c_normed, c_nhi, c_nlo, c_ob = (sig("c_mean", 2 * TT), sig("c_rstd", 2), sig("c_normed", TT),
                                                        sig("c_nhi"), sig("c_nlo"), sig("c_ob"))
        c_rscore, c_sbc, c_before, c_rank, c_selt, c_seltp, c_sel, c_xs, c_xput, c_sqs, c_rms_s = (
            sig("c_rscore", TT), sig("c_sbc"), sig("c_before", 2 * TT), sig("c_rank"), sig("c_selt"),
            sig("c_seltp"), sig("c_sel"), sig("c_xs"), sig("c_xput"), sig("c_sqs"), sig("c_rms_s", 2))
        c_h, c_htp, c_hput, c_hhi, c_hlo, c_qk, c_v, c_qkput, c_vput = (
            sig("c_h"), sig("c_htp"), sig("c_hput", DC), sig("c_hhi"), sig("c_hlo"), sig("c_qk"), sig("c_v"),
            sig("c_qkput", 3), sig("c_vput", 2))
        c_score, c_smask, c_exp, c_etp, c_etput, c_att = (
            sig("c_score", 4), sig("c_smask", 8), sig("c_exp", 16), sig("c_etp", 4), sig("c_etput", 4), sig("c_att", 4))
        c_dinv, c_dtp, c_dput, c_o, c_ohi, c_olo, c_xo, c_xoput = (
            sig("c_dinv", 3), sig("c_dtp"), sig("c_dput"), sig("c_o"), sig("c_ohi"), sig("c_olo"), sig("c_xo"),
            sig("c_xoput"))
        c_h2s, c_h2sq, c_h2rms, c_h2n_s, c_h2tp, c_h2put, c_h2hi, c_h2lo = (
            sig("c_h2s"), sig("c_h2sq"), sig("c_h2rms", 2), sig("c_h2n_s"), sig("c_h2tp"), sig("c_h2put", DC),
            sig("c_h2hi"), sig("c_h2lo"))
        c_gu, c_tanh, c_gate, c_gtp, c_gthi, c_gtlo, c_ff, c_y, c_yhi, c_ylo, c_scat, c_done = (
            sig("c_gu", 2), sig("c_tanh", 2), sig("c_gate", 4), sig("c_gtp", 2), sig("c_gthi", 2), sig("c_gtlo", 2),
            sig("c_ff"), sig("c_y"), sig("c_yhi"), sig("c_ylo"), sig("c_scat"), sig("c_done"))
        passed = sig("passed")

        def rows_of(t):
            return t.rearrange("(b t p) d -> b p t d", b=B, p=P)

        x_rows, ctx_rows, out_rows = rows_of(x), rows_of(ctx_in), rows_of(out)

        block = ctx.enter_context(nc.Block())

        def named(*steps):
            return {f.__name__.rstrip("_"): f for f in steps}

        def flat(a):
            return a.rearrange("p a b -> p (a b)")

        def heads(a):
            return a.rearrange("p (h q) -> p h q", h=4)

        def parity(a, m):
            return a.rearrange("p (n m e) -> p n m e", m=2, e=HD)[:, :, m, :]

        def logits(g):
            return (c_norm, c_odd)[g % 2]

        @block.sync
        def _(sp):
            sp.dma_start(const[:, :], consts).then_inc(const_in.sem, 16)
            sp.dma_start(xin[:, :, :], x_rows[0]).then_inc(x_in.sem, 16)

            for n in range(NRAW):
                sp.dma_start(raw[:, n, 0:loads[n][1]], loads[n][0]).then_inc(raw_in[n].sem, 16)
            sp.dma_start(qc[:, TT:2 * TT, :], ctx_rows[0]).then_inc(ctx_in_s.sem, 16)
            sp.dma_start(bc[:, :, :], vec_bc).then_inc(vec_in.sem, 16)
            sp.dma_start(cols[:, :], vec_cols).then_inc(vec_in.sem, 16)
            sp.dma_start(wcqk[:, :, :], w_cqk).then_inc(qk_in.sem, 16)

            def next_x(b):
                sp.wait_ge(*a_normed(b))
                sp.sem_inc(passed.sem, 1)
                sp.wait_ge(*a_kept(b))
                sp.sem_inc(passed.sem, 1)
                sp.dma_start(xin[:, :, :], x_rows[b + 1]).then_inc(x_in.sem, 16)

            def next_ctx(b):
                sp.wait_ge(*b_tanh(b))
                sp.wait_ge(*b_chi(b))
                sp.wait_ge(*b_clo(b))
                sp.sem_inc(passed.sem, 1)
                sp.dma_start(qc[:, TT:2 * TT, :], ctx_rows[b + 1]).then_inc(ctx_in_s.sem, 16)

            def store(b):
                sp.wait_ge(*c_done(b))
                sp.sem_inc(passed.sem, 1)
                sp.dma_start(out_rows[b], ob[:, :, :]).then_inc(out_done.sem, 16)

            next_x(0)
            next_x(1)
            next_ctx(0)
            next_x(2)
            next_ctx(1)
            store(0)
            with sp.Fori(3, B - 1) as i:
                next_x(i)
                next_ctx(i - 1)
                store(i - 2)
            next_ctx(B - 2)
            store(B - 3)
            store(B - 2)
            store(B - 1)
            sp.wait_ge(*out_done(B - 1))

        @block.gpsimd
        def _(pool):
            nc.gpsimd.memset(ones_bf[:, :], 1.0).then_inc(ones_set.sem, 1)
            pool.wait_ge(const_in.sem, 16)
            add_bc = lambda out_, in_, vec: nc.gpsimd.tensor_tensor(
                out_, in_, vec.unsqueeze(1).broadcast_to([P, TT, D]), ALU.add)

            def power(b, source, in_, eps, out_, done):
                pool.wait_ge(*source(b))
                pool.sem_inc(passed.sem, 1)
                nc.gpsimd.tensor_scalar(out_, in_, eps, None, ALU.add).then_inc(done.sem, 1)
                pool.wait_ge(*done(b, 1))
                nc.gpsimd.tensor_tensor(out_, out_, C["minus_half"][:, 0:out_.shape[1]], ALU.pow).then_inc(done.sem, 1)

            def a_rstd_(b):
                power(b, a_mean, a_mv[:, :, 1], LN_EPS, a_rs[:, :], a_rstd)

            def a_kept_(b):
                if not first(b):
                    pool.wait_ge(*b_kept(b - 1))
                    pool.wait_ge(*b_normed(b - 1))
                pool.wait_ge(*x_in(b))
                pool.sem_inc(passed.sem, 1)
                nc.gpsimd.tensor_copy(x1[:, :, :], xin[:, :, :]).then_inc(a_kept.sem, 1)

            def a_rden_(b):
                pool.wait_ge(*a_dinv(b))
                pool.sem_inc(passed.sem, 1)
                pool.wait_ge(*a_phi(b))
                pool.sem_inc(passed.sem, 1)
                nc.gpsimd.tensor_copy(a_e1[:, :].rearrange("p (n e) -> p n e", e=HD),
                                      a_r[:, :].unsqueeze(2).broadcast_to([P, TT * NH, HD])).then_inc(a_rden.sem, 1)

            def b_rstd_(b):
                power(b, b_mean, b_mv[:, :, 1], LN_EPS, b_rs[:, :], b_rstd)

            def b_kept_(b):
                pool.wait_ge(*a_done(b))
                if not first(b):
                    pool.wait_ge(*c_ob(b - 1))
                    pool.wait_ge(*c_normed(b - 1))
                else:
                    pool.wait_ge(vec_in.sem, 32)
                add_bc(x2[:, :, :], x1[:, :, :], ln_b_bc).then_inc(b_kept.sem, 1)

            def b_clo_(b):
                pool.wait_ge(*b_chi(b))
                nc.gpsimd.tensor_tensor(b_s2[1][:, :], flat(qc[:, TT:2 * TT, :]), b_s2[0][:, :].bitcast(F32),
                                        ALU.subtract).then_inc(b_clo.sem, 1)

            def b_qb_(b):
                pool.wait_ge(*b_normed(b))
                if not first(b):
                    pool.wait_ge(*b_o(b - 1))
                add_bc(qb[:, :, :], qc[:, 0:TT, :], b_diff_bc).then_inc(b_qb.sem, 1)

            def b_frstd_(b):
                power(b, b_fmean, f_mv[:, :, 1], LN_EPS, f_rs[:, :], b_frstd)

            def b_fb2_(b):
                pool.wait_ge(*b_fput(b))
                add_bc(qb[:, :, :], b_f0[:, :, :], b2_bc).then_inc(b_fb2.sem, 1)

            def b_orstd_(b):
                power(b, b_omean, f_mv[:, :, 1], LN_EPS, f_rs[:, :], b_orstd)

            def c_rstd_(b):
                power(b, c_mean, c_mv[:, :, 1], LN_EPS, c_rs[:, :], c_rstd)

            def c_ob_(b):
                pool.wait_ge(*c_normed(b))
                if not first(b):
                    pool.wait_ge(*out_done(b - 1))
                nc.gpsimd.tensor_tensor(ob[:, :, :], x2[:, :, :], c_norm[:, :, :], ALU.add).then_inc(c_ob.sem, 1)

            def c_nlo_(b):
                pool.wait_ge(*c_nhi(b))
                nc.gpsimd.tensor_tensor(flat(act_t[1][:, 0:4, :]), flat(c_norm[:, :, :]),
                                        flat(act_t[0][:, 0:4, :]).bitcast(F32), ALU.subtract).then_inc(c_nlo.sem, 1)

            def c_rms_(b):
                power(b, c_sqs, c_sq[:, :], RMS_EPS, c_rms[:, :], c_rms_s)

            def c_h2rms_(b):
                power(b, c_h2sq, c_sq2[:, :], RMS_EPS, c_rms2[:, :], c_h2rms)

            rounds(pool, named(a_rstd_, a_kept_, b_rstd_, b_kept_, b_clo_, b_qb_, b_frstd_, b_fb2_, b_orstd_, c_rstd_,
                               c_ob_, c_nlo_, c_rms_, c_h2rms_, a_rden_))

        @block.scalar
        def _(act_e):
            act_in = nc.scalar.activation

            def copy(out_, in_, done, scale=1.0):
                act_in(out_, in_, ACT.Copy, scale=scale).then_inc(done.sem, 1)

            upcoming = iter(range(len(loads)))

            def split_weights(count):
                for _ in range(count):
                    n = next(upcoming)
                    act_e.wait_ge(raw_in[n % NRAW].sem, 16 * (n // NRAW + 1))
                    copy(loads[n][2][0], raw[:, n % NRAW, 0:loads[n][1]], raw_hi)
                    after = n - 1 + NRAW
                    if NRAW <= after < len(loads):
                        act_e.wait_ge(raw_hi.sem, n)
                        act_e.wait_ge(raw_lo.sem, n)
                        act_e.dma_start(raw[:, after % NRAW, 0:loads[after][1]], loads[after][0]) \
                            .then_inc(raw_in[after % NRAW].sem, 16)

            def a_thi_(b):
                act_e.wait_ge(*a_tp(b))
                if not first(b):
                    act_e.wait_ge(*a_proj(b - 1))
                copy(flat(a_tr[0][:, :, :]), a0[:, :], a_thi)

            def a_qout_(b):
                act_e.wait_ge(*a_qk(b, 1))
                act_in(a_e0[:, :], a1[:, :], ACT.Exp).then_inc(a_qout.sem, 1)
                act_in(flat(qT[:, :, :]), a1[:, :], ACT.Relu).then_inc(a_qout.sem, 1)

            def a_kout_(b):
                act_e.wait_ge(*a_qk(b))
                act_in(a_e1[:, :], a2[:, :], ACT.Exp).then_inc(a_kout.sem, 1)
                act_in(flat(kT[:, :, :]), a2[:, :], ACT.Relu).then_inc(a_kout.sem, 1)

            def kv_out(t):
                def step(b):
                    bk = (a0, a1)[t]
                    act_e.wait_ge(*a_kv(b, t + 1))
                    act_in(a_s1[:, t * D:(t + 1) * D], bk[:, 0:D], ACT.Exp).then_inc(a_kvout.sem, 1)
                    act_in(k_tok[:, t, :], bk[:, 0:D], ACT.Relu).then_inc(a_kvout.sem, 1)
                    for m in range(2):
                        copy(parity(vM[m][:, t, :], m), parity(bk[:, D:2 * D], m), a_v)
                    if t == 0:
                        copy(v0[:, :], bk[:, D:2 * D], a_v)
                return step

            def a_mask_(b):
                act_e.wait_ge(*a_phi(b, 1))
                for m, mask in enumerate(("even", "odd")):
                    copy(qM[:, :, :, m, :], qT[:, :, :].rearrange("p c (t q) -> p c t q", t=TT), a_mask, C[mask])

            def a_dput_(b):
                act_e.wait_ge(*a_rtp(b))
                copy(a_e1[:, :], a0[:, :], a_dput)

            def a_yhi_(b):
                act_e.wait_ge(*a_y(b))
                copy(a_tr[0][:, :, :], a_norm[:, :, :], a_yhi)

            def b_chi_(b):
                act_e.wait_ge(*ctx_in_s(b))
                if not first(b):
                    act_e.wait_ge(*b_down(b - 1))
                copy(b_s2[0][:, :], flat(qc[:, TT:2 * TT, :]), b_chi)

            def b_tanh_(b):
                if first(b):
                    act_e.wait_ge(vec_in.sem, 32)
                act_e.wait_ge(*b_normed(b))
                act_e.wait_ge(*ctx_in_s(b))
                if not first(b):
                    act_e.wait_ge(*b_glo(b - 1))
                    act_e.wait_ge(*b_ghi(b - 1))
                act_in(prob[:, :, :], qc[:, :, :], ACT.Tanh).then_inc(b_tanh.sem, 1)

            def b_praw_(b):
                act_e.wait_ge(*b_tanh(b))
                for s in range(2 * TT):
                    act_in(prob[:, s, :], prob[:, s, :], ACT.Identity, bias=C["prob_bias"], scale=0.499,
                           accum_out=b_sum[:, s:s + 1]).then_inc(b_praw.sem, 1)

            def b_log_(b):
                act_e.wait_ge(*b_diff(b))
                act_in(prob[:, :, :], prob[:, :, :], ACT.Ln).then_inc(b_log.sem, 1)

            def b_dhi_(b):
                act_e.wait_ge(*b_pairtp(b, 1))
                copy(b_s0[0][:, :], b0[:, :], b_pairhi)

            def b_rhi_(b):
                act_e.wait_ge(*b_pairtp(b))
                copy(b_s1[0][:, :], b1[:, :], b_pairhi)

            def b_sexp_(b):
                act_e.wait_ge(*b_sbias(b))
                for t in range(TT):
                    act_in(prob[:, t, :], b0[:, t * T:(t + 1) * T], ACT.Exp, bias=b_bias[:, t:t + 1],
                           scale=-1.0 / D ** 0.5, accum_out=b_z[:, t:t + 1]).then_inc(b_sexp.sem, 1)

            def b_ahi_(b):
                act_e.wait_ge(*b_atp(b))
                copy(b_s0[0][:, :], b1[:, :], b_ahi)

            def b_fdhi_(b):
                act_e.wait_ge(*b_fd(b))
                copy(b_s1[0][:, :], b0[:, :], b_fdhi)

            def b_hhi_(b):
                act_e.wait_ge(*b_haff(b))
                copy(b_s0[0][:, :], flat(b_f1[:, :, :]), b_hhi)

            def gelu(j):
                def step(b):
                    act_e.wait_ge(*b_up(b, j + 1))
                    if j >= 2:
                        act_e.wait_ge(*b_glo(b, j - 1))
                    for n in range(2):
                        f = 2 * j + n
                        act_in(prob[:, 2 * (j % 2) + n, :], b0[:, n * T:(n + 1) * T], ACT.Gelu,
                               bias=b1_col[:, f:f + 1]).then_inc(b_gelu.sem, 1)
                return step

            def gelu_hi(j):
                def step(b):
                    act_e.wait_ge(*b_gelu(b, 2 * j + 2))
                    if j >= 2:
                        act_e.wait_ge(*b_down(b, j - 1))
                    copy((b_s2, b_s1)[j % 2][0][:, :], flat(prob[:, 2 * (j % 2):2 * (j % 2) + 2, :]), b_ghi)
                return step

            def c_nhi_(b):
                act_e.wait_ge(*c_normed(b))
                if not first(b):
                    act_e.wait_ge(*c_ff(b - 1))
                copy(flat(act_t[0][:, 0:4, :]), flat(c_norm[:, :, :]), c_nhi)

            def c_sel_(b):
                act_e.wait_ge(*c_seltp(b))
                copy(flat(sel[:, :, :]), c2[:, 0:T], c_sel)

            def c_xput_(b):
                act_e.wait_ge(*c_xs(b))
                act_in(c_h2n[:, :], c1[:, 0:D], ACT.Square, scale=1.0 / D ** 0.5, accum_out=c_sq[:, :]) \
                    .then_inc(c_sqs.sem, 1)
                copy(x_sel[:, :], c1[:, 0:D], c_xput)

            def c_h_(b):
                act_e.wait_ge(*c_rms_s(b))
                act_e.wait_ge(*c_xput(b))
                copy(c_h2[:, :], x_sel[:, :], c_h, c_rms[:, :])

            def c_hhi_(b):
                act_e.wait_ge(*c_hput(b))
                copy(c_hs[0][:, :, :], c_hT[:, :, :], c_hhi)

            def c_qkput_(b):
                act_e.wait_ge(*c_qk(b))
                copy(flat(cq[:, :, :]), c2[:, 0:2 * R], c_qkput, 1.0 / HD ** 0.5)
                for m, mask in enumerate(("even", "odd")):
                    copy(ck[:, :, m, :], c2[:, 2 * R:4 * R].rearrange("p (c r) -> p c r", c=DC), c_qkput, C[mask])

            def c_vput_(b):
                act_e.wait_ge(*c_v(b))
                for m in range(2):
                    copy(parity(cv[m][:, :], m), parity(c0[:, 0:D], m), c_vput)

            def c_exp_(g):
                def step(b):
                    act_e.wait_ge(*c_smask(b, 2 * g + 2))
                    for j in range(4):
                        h = flat(logits(g)[:, :, :])[:, j * R:(j + 1) * R]
                        n = 4 * g + j
                        act_in(h, h, ACT.Exp, bias=c_nmax[:, n:n + 1], accum_out=c_den[:, n:n + 1]) \
                            .then_inc(c_exp.sem, 1)
                return step

            def c_etput_(g):
                def step(b):
                    act_e.wait_ge(*c_etp(b, g + 1))
                    if g >= 2:
                        act_e.wait_ge(*c_att(b, g - 1))
                    copy(c_et[g % 2][:, :], (c1, c2)[g % 2][:, :], c_etput)
                return step

            def c_dput_(b):
                act_e.wait_ge(*c_dtp(b))
                act_e.wait_ge(*c_att(b))
                copy(c_rT[:, :], c0[:, D:2 * D], c_dput)

            def c_ohi_(b):
                act_e.wait_ge(*c_o(b))
                copy(c_hs[0][:, :, :], c_hT[:, :, :], c_ohi)

            def c_xoput_(b):
                act_e.wait_ge(*c_xo(b))
                copy(x_att[:, :], c0[:, 0:D], c_xoput)

            def c_h2sq_(b):
                act_e.wait_ge(*c_h2s(b))
                act_in(c_h2n[:, :], c_h2[:, :], ACT.Square, scale=1.0 / D ** 0.5, accum_out=c_sq2[:, :]) \
                    .then_inc(c_h2sq.sem, 1)

            def c_h2n_(b):
                act_e.wait_ge(*c_h2rms(b))
                copy(c_h2n[:, :], c_h2[:, :], c_h2n_s, c_rms2[:, :])

            def c_h2hi_(b):
                act_e.wait_ge(*c_h2put(b))
                copy(c_hs[0][:, :, :], c_hT[:, :, :], c_h2hi)

            def c_tanh_(j):
                def step(b):
                    n = (FG, FF - FG)[j]
                    act_e.wait_ge(*c_gu(b, j + 1))
                    if j:
                        act_e.wait_ge(*c_gate(b, 2))
                    act_in(c_et[0][:, 0:n], c1[:, 0:n], ACT.Tanh, scale=0.5).then_inc(c_tanh.sem, 1)
                return step

            def c_gthi_(j):
                def step(b):
                    bk, s = ((c1, slice(0, 4)), (c2, slice(4, 6)))[j]
                    act_e.wait_ge(*c_gtp(b, j + 1))
                    copy(flat(act_t[0][:, s, :]), bk[:, 0:(s.stop - s.start) * R], c_gthi)
                return step

            def c_yhi_(b):
                act_e.wait_ge(*c_y(b))
                copy(flat(c_hs[0][:, :, :]), c_h2[:, :], c_yhi)

            act_e.wait_ge(const_in.sem, 16)
            rounds(act_e, named(a_thi_, a_qout_, a_kout_, a_mask_, a_dput_, a_yhi_, b_chi_, b_tanh_, b_praw_, b_log_, b_dhi_,
                                b_rhi_, b_sexp_, b_ahi_, b_fdhi_, b_hhi_, c_nhi_, c_sel_, c_xput_, c_h_, c_hhi_,
                                c_qkput_, c_vput_, c_dput_, c_ohi_, c_xoput_, c_h2sq_, c_h2n_, c_h2hi_, c_yhi_)
                   | {f"a_kvout_{t}": kv_out(t) for t in range(TT)}
                   | {f"b_gelu_{j}": gelu(j) for j in range(4)} | {f"b_ghi_{j}": gelu_hi(j) for j in range(4)}
                   | {f"c_exp_{g}": c_exp_(g) for g in range(4)} | {f"c_etput_{g}": c_etput_(g) for g in range(4)}
                   | {f"c_tanh_{j}": c_tanh_(j) for j in range(2)} | {f"c_gthi_{j}": c_gthi_(j) for j in range(2)},
                   split_weights)

        @block.vector
        def _(dve):
            ts, tt, stt = nc.vector.tensor_scalar, nc.vector.tensor_tensor, nc.vector.scalar_tensor_tensor

            upcoming = iter(range(len(loads)))

            def split_weights(count):
                for _ in range(count):
                    n = next(upcoming)
                    dve.wait_ge(raw_hi.sem, n + 1)
                    tt(loads[n][2][1], raw[:, n % NRAW, 0:loads[n][1]], loads[n][2][0].bitcast(F32),
                       ALU.subtract).then_inc(raw_lo.sem, 1)

            def low(out_, full, high, done):
                tt(out_, full, high.bitcast(F32), ALU.subtract).then_inc(done.sem, 1)

            def statistics(b, src, st, mv, mean):
                for t in range(TT):
                    nc.vector.bn_stats(st[:, t, :], src[:, t, :]).then_inc(mean.sem, 1)
                for t in range(TT):
                    dve.wait_ge(*mean(b, t + 1))
                    dve.sem_inc(passed.sem, 1)
                    nc.vector.bn_aggr(mv[:, t, :], st[:, t, :]).then_inc(mean.sem, 1)

            def normalise(b, dst, src, mv, rs, rstd, normed):
                dve.wait_ge(*rstd(b))
                for t in range(TT):
                    ts(dst[:, t, :], src[:, t, :], mv[:, t, 0:1], rs[:, t:t + 1], ALU.subtract, ALU.mult) \
                        .then_inc(normed.sem, 1)

            def a_mean_(b):
                dve.wait_ge(*x_in(b))
                if not first(b):
                    dve.wait_ge(*a_normed(b - 1))
                statistics(b, xin, a_st, a_mv, a_mean)

            def a_normed_(b):
                if not first(b):
                    dve.wait_ge(*a_yhi(b - 1))
                    dve.wait_ge(*a_ylo(b - 1))
                normalise(b, a_norm, xin, a_mv, a_rs, a_rstd, a_normed)

            def a_tlo_(b):
                dve.wait_ge(*a_thi(b))
                low(flat(a_tr[1][:, :, :]), a0[:, :], flat(a_tr[0][:, :, :]), a_tlo)

            def phi(out_, e, done):
                stt(out_, e, 1.0, out_, ALU.min, ALU.add).then_inc(done.sem, 1)

            def a_phi_q_(b):
                dve.wait_ge(*a_qout(b))
                phi(flat(qT[:, :, :]), a_e0[:, :], a_phi)

            def a_phi_k_(b):
                dve.wait_ge(*a_kout(b))
                phi(flat(kT[:, :, :]), a_e1[:, :], a_phi)

            def k_phi(t):
                def step(b):
                    dve.wait_ge(*a_kvout(b, 2 * (t + 1)))
                    phi(k_tok[:, t, :], a_s1[:, t * D:(t + 1) * D], a_kphi)
                return step

            def a_sput_(b):
                dve.wait_ge(*a_state(b))
                tt(state[:, :].rearrange("p (c e) -> p c e", c=DC), a2[:, 0:D].rearrange("p (c e) -> p c e", c=DC),
                   C["head_block"].unsqueeze(1).broadcast_to([P, DC, P]), ALU.mult).then_inc(a_sput.sem, 1)

            def a_kq_(b):
                dve.wait_ge(*a_ksum(b))
                tt(a_e0[:, :], a0[:, :], flat(qT[:, :, :]), ALU.mult).then_inc(a_kq.sem, 1)

            def a_dinv_(b):
                dve.wait_ge(*a_den(b))
                ts(a_r[:, :], a0[:, 0:TT * NH], DEN_EPS, None, ALU.add).then_inc(a_dinv.sem, 1)
                dve.wait_ge(*a_dinv(b, 1))
                nc.vector.reciprocal(a_r[:, :], a_r[:, :]).then_inc(a_dinv.sem, 1)

            def a_scput_(g):
                def step(b):
                    dve.wait_ge(*a_score(b, g + 1))
                    if g == 0:
                        dve.wait_ge(*a_kphi(b))
                    if g == 1:
                        dve.wait_ge(*a_den(b))
                    if g >= 2:
                        dve.wait_ge(*a_att(b, g - 1))
                    tt(heads((a_s1, a_e0)[g % 2][:, :]), heads((a1, a2)[g % 2][:, :]),
                       tri.unsqueeze(1).broadcast_to([P, 4, P]), ALU.mult).then_inc(a_scput.sem, 1)
                return step

            def a_y_(b):
                dve.wait_ge(*a_att(b))
                dve.wait_ge(*a_dput(b))
                tt(flat(a_norm[:, :, :]), a0[:, :], a_e1[:, :], ALU.mult).then_inc(a_y.sem, 1)

            def a_ylo_(b):
                dve.wait_ge(*a_yhi(b))
                dve.wait_ge(*a_y(b))
                low(a_tr[1][:, :, :], a_norm[:, :, :], a_tr[0][:, :, :], a_ylo)

            def a_done_(b):
                dve.wait_ge(*a_proj(b))
                dve.wait_ge(*a_kept(b))
                tt(flat(x1[:, :, :]), flat(x1[:, :, :]), a1[:, :], ALU.add).then_inc(a_done.sem, 1)

            def b_mean_(b):
                dve.wait_ge(*a_done(b))
                if first(b):
                    dve.wait_ge(vec_in.sem, 32)
                if not first(b):
                    dve.wait_ge(*b_normed(b - 1))
                statistics(b, x1, b_st, b_mv, b_mean)

            def b_normed_(b):
                if not first(b):
                    dve.wait_ge(*b_tanh(b - 1))
                    dve.wait_ge(*b_qb(b - 1))
                normalise(b, qc, x1, b_mv, b_rs, b_rstd, b_normed)

            def b_pnorm_(b):
                dve.wait_ge(*b_praw(b))
                ts(b_rsum[:, :], b_sum[:, :], PROB_EPS, None, ALU.add).then_inc(b_rsum_s.sem, 1)
                dve.wait_ge(*b_rsum_s(b, 1))
                nc.vector.reciprocal(b_rsum[:, :], b_rsum[:, :]).then_inc(b_rsum_s.sem, 1)
                dve.wait_ge(*b_rsum_s(b))
                for s in range(2 * TT):
                    ts(prob[:, s, :], prob[:, s, :], b_rsum[:, s:s + 1], PROB_EPS, ALU.mult, ALU.max) \
                        .then_inc(b_pnorm.sem, 1)

            def b_diff_(b):
                dve.wait_ge(*b_pnorm(b))
                if not first(b):
                    dve.wait_ge(*b_done(b - 1))
                tt(b_f0[:, :, :], prob[:, 0:TT, :], prob[:, TT:2 * TT, :], ALU.subtract).then_inc(b_diff.sem, 1)

            def b_ratio_(b):
                dve.wait_ge(*b_log(b))
                tt(b_f1[:, :, :], prob[:, 0:TT, :], prob[:, TT:2 * TT, :], ALU.subtract).then_inc(b_ratio.sem, 1)

            def b_dlo_(b):
                dve.wait_ge(*b_pairhi(b, 1))
                low(b_s0[1][:, :], b0[:, :], b_s0[0][:, :], b_pairlo)

            def b_rlo_(b):
                dve.wait_ge(*b_pairhi(b))
                low(b_s1[1][:, :], b1[:, :], b_s1[0][:, :], b_pairlo)

            def b_sbias_(b):
                dve.wait_ge(*b_sid(b))
                nc.vector.tensor_reduce(b_min[:, :], b0[:, :].rearrange("p (t m) -> p t m", t=TT), axis=AX.X,
                                        op=ALU.min).then_inc(b_sbias.sem, 1)
                dve.wait_ge(*b_sbias(b, 1))
                ts(b_bias[:, :], b_min[:, :], 1.0 / D ** 0.5, None, ALU.mult).then_inc(b_sbias.sem, 1)

            def b_attn_(b):
                dve.wait_ge(*b_sexp(b))
                nc.vector.reciprocal(b_z[:, :], b_z[:, :]).then_inc(b_zinv.sem, 1)
                dve.wait_ge(*b_zinv(b))
                for t in range(TT):
                    stt(prob[:, TT + t, :], prob[:, t, :], b_z[:, t:t + 1], ident2[:, t, :], ALU.mult, ALU.subtract,
                        reverse1=True).then_inc(b_attn.sem, 1)

            def b_alo_(b):
                dve.wait_ge(*b_ahi(b))
                low(b_s0[1][:, :], b1[:, :], b_s0[0][:, :], b_alo)

            def b_fdlo_(b):
                dve.wait_ge(*b_fdhi(b))
                low(b_s1[1][:, :], b0[:, :], b_s1[0][:, :], b_fdlo)

            def b_fput_(b):
                dve.wait_ge(*b_f(b))
                dve.wait_ge(*b_qb(b))
                tt(flat(b_f0[:, :, :]), b1[:, :], flat(qb[:, :, :]), ALU.add).then_inc(b_fput.sem, 1)

            def b_fmean_(b):
                dve.wait_ge(*b_fput(b))
                statistics(b, b_f0, f_st, f_mv, b_fmean)

            def b_fnormed_(b):
                normalise(b, prob, b_f0, f_mv, f_rs, b_frstd, b_fnormed)

            def b_haff_(b):
                dve.wait_ge(*b_htp(b))
                for c in range(DC):
                    ts(b_f1[:, c, :], b0[:, c * T:(c + 1) * T], ln_g_col[:, c:c + 1], ln_b_col[:, c:c + 1], ALU.mult,
                       ALU.add).then_inc(b_haff.sem, 1)

            def b_hlo_(b):
                dve.wait_ge(*b_hhi(b))
                dve.wait_ge(*b_haff(b))
                low(b_s0[1][:, :], flat(b_f1[:, :, :]), b_s0[0][:, :], b_hlo)

            def gelu_lo(j):
                def step(b):
                    hi, lo = (b_s2, b_s1)[j % 2]
                    dve.wait_ge(*b_ghi(b, j + 1))
                    low(lo[:, :], flat(prob[:, 2 * (j % 2):2 * (j % 2) + 2, :]), hi[:, :], b_glo)
                return step

            def b_o_(b):
                dve.wait_ge(*b_down(b))
                dve.wait_ge(*b_fb2(b))
                tt(flat(b_f0[:, :, :]), b1[:, :], flat(qb[:, :, :]), ALU.add).then_inc(b_o.sem, 1)

            def b_omean_(b):
                dve.wait_ge(*b_o(b))
                statistics(b, b_f0, f_st, f_mv, b_omean)

            def b_onormed_(b):
                normalise(b, b_f0, b_f0, f_mv, f_rs, b_orstd, b_onormed)

            def b_done_(b):
                dve.wait_ge(*b_onormed(b))
                tt(b_f0[:, :, :], b_f0[:, :, :], ln_g_bc.unsqueeze(1).broadcast_to([P, TT, D]), ALU.mult) \
                    .then_inc(b_ogain.sem, 1)
                dve.wait_ge(*b_ogain(b))
                dve.wait_ge(*b_kept(b))
                tt(x2[:, :, :], x2[:, :, :], b_f0[:, :, :], ALU.add).then_inc(b_done.sem, 1)

            def c_mean_(b):
                dve.wait_ge(*b_done(b))
                if first(b):
                    dve.wait_ge(raw_lo.sem, len(loads))
                else:
                    dve.wait_ge(*c_normed(b - 1))
                statistics(b, x2, c_st, c_mv, c_mean)

            def c_normed_(b):
                if not first(b):
                    dve.wait_ge(*c_etp(b - 1, 3))
                    dve.wait_ge(*c_ob(b - 1))
                normalise(b, c_norm, x2, c_mv, c_rs, c_rstd, c_normed)

            def c_rscore_(b):
                for t in range(TT):
                    dve.wait_ge(*c_normed(b, t + 1))
                    nc.vector.tensor_tensor_reduce(out=tie[:, :], in0=c_norm[:, t, :], in1=router_bc, scale=1.0,
                                                   scalar=0.0, op0=ALU.mult, op1=ALU.add,
                                                   accum_out=c_sc[:, t:t + 1]).then_inc(c_rscore.sem, 1)
                    dve.wait_ge(*c_rscore(b, t + 1))

            def c_before_(b):
                dve.wait_ge(*c_sbc(b))
                for t in range(TT):
                    if t:
                        dve.wait_ge(*c_before(b, 2 * t))
                    stt(tie[:, :], c0[:, 0:T], c_sc[:, t:t + 1], tie_mask[:, t, :], ALU.is_equal, ALU.mult) \
                        .then_inc(c_before.sem, 1)
                    dve.wait_ge(*c_before(b, 2 * t + 1))
                    stt(before[:, t, :], c0[:, 0:T], c_sc[:, t:t + 1], tie[:, :], ALU.is_lt, ALU.add) \
                        .then_inc(c_before.sem, 1)

            def c_selt_(b):
                dve.wait_ge(*c_rank(b))
                ts(sel_t[:, :], c1[:, 0:T], C["iota"], None, ALU.is_equal).then_inc(c_selt.sem, 1)

            def gain(b, source, bk, col, done):
                dve.wait_ge(*source(b))
                for c in range(DC):
                    ts(c_hT[:, c, :], bk[:, c * R:(c + 1) * R], col[:, c:c + 1], None, ALU.mult).then_inc(done.sem, 1)

            def c_hput_(b):
                gain(b, c_htp, c0, g1_col, c_hput)

            def c_hlo_(b):
                dve.wait_ge(*c_hhi(b))
                dve.wait_ge(*c_hput(b))
                low(c_hs[1][:, :, :], c_hT[:, :, :], c_hs[0][:, :, :], c_hlo)

            def c_smask_(g):
                def step(b):
                    x = heads(flat(logits(g)[:, :, :]))
                    dve.wait_ge(*c_score(b, g + 1))
                    if g == 0:
                        dve.wait_ge(*c_ob(b))
                    if g >= 2:
                        dve.wait_ge(*c_etp(b, g - 1))
                    tt(x, heads((c1, c2)[g % 2][:, :]), neg_mask.unsqueeze(1).broadcast_to([P, 4, R]), ALU.add) \
                        .then_inc(c_smask.sem, 1)
                    dve.wait_ge(*c_smask(b, 2 * g + 1))
                    nc.vector.tensor_reduce(c_nmax[:, 4 * g:4 * g + 4], x, axis=AX.X, op=ALU.max, negate=True) \
                        .then_inc(c_smask.sem, 1)
                return step

            def c_dinv_(b):
                dve.wait_ge(*c_exp(b))
                nc.vector.reciprocal(c_den[:, :], c_den[:, :]).then_inc(c_dinv.sem, 1)
                dve.wait_ge(*c_dinv(b, 1))
                for c in range(DC):
                    nc.vector.tensor_copy(
                        c_rden[:, c * P:(c + 1) * P].rearrange("p (g m e) -> p g m e", m=2, e=HD),
                        c_den[:, :].rearrange("p (g c m) -> p g c m", c=DC, m=2)[:, :, c, :].unsqueeze(3)
                        .broadcast_to([P, NH // 4, 2, HD])).then_inc(c_dinv.sem, 1)

            def c_o_(b):
                dve.wait_ge(*c_dput(b))
                dve.wait_ge(*c_att(b))
                tt(flat(c_hT[:, :, :]), c0[:, 0:D], c_rT[:, :], ALU.mult).then_inc(c_o.sem, 1)

            def c_olo_(b):
                dve.wait_ge(*c_ohi(b))
                dve.wait_ge(*c_o(b))
                low(c_hs[1][:, :, :], c_hT[:, :, :], c_hs[0][:, :, :], c_olo)

            def c_h2s_(b):
                dve.wait_ge(*c_xoput(b))
                dve.wait_ge(*c_xput(b))
                tt(c_h2[:, :], c0[:, 0:D], x_sel[:, :], ALU.add).then_inc(c_h2s.sem, 1)

            def c_h2put_(b):
                gain(b, c_h2tp, c1, g2_col, c_h2put)

            def c_h2lo_(b):
                dve.wait_ge(*c_h2hi(b))
                dve.wait_ge(*c_h2put(b))
                low(c_hs[1][:, :, :], c_hT[:, :, :], c_hs[0][:, :, :], c_h2lo)

            def c_gate_(j):
                def step(b):
                    n = (FG, FF - FG)[j]
                    half, val = c_et[0][:, 0:n], c_et[1][:, 0:n]
                    dve.wait_ge(*c_tanh(b, j + 1))
                    if j:
                        dve.wait_ge(*c_gate(b, 2))
                    stt(val, half, 1.0, c1[:, 0:n], ALU.add, ALU.mult).then_inc(c_gate.sem, 1)
                    dve.wait_ge(*c_gate(b, 2 * j + 1))
                    stt(act[:, j * FG:j * FG + n], val, 0.5, c2[:, 0:n], ALU.mult, ALU.mult).then_inc(c_gate.sem, 1)
                return step

            def c_gtlo_(j):
                def step(b):
                    bk, s = ((c1, slice(0, 4)), (c2, slice(4, 6)))[j]
                    dve.wait_ge(*c_gthi(b, j + 1))
                    low(flat(act_t[1][:, s, :]), bk[:, 0:(s.stop - s.start) * R], flat(act_t[0][:, s, :]), c_gtlo)
                return step

            def c_y_(b):
                dve.wait_ge(*c_ff(b))
                dve.wait_ge(*c_xoput(b))
                tt(c_h2[:, :], c0[:, D:2 * D], x_att[:, :], ALU.add).then_inc(c_y.sem, 1)

            def c_ylo_(b):
                dve.wait_ge(*c_yhi(b))
                dve.wait_ge(*c_y(b))
                low(flat(c_hs[1][:, :, :]), c_h2[:, :], flat(c_hs[0][:, :, :]), c_ylo)

            def c_done_(b):
                dve.wait_ge(*c_scat(b))
                dve.wait_ge(*c_ob(b))
                tt(flat(ob[:, :, :]), flat(ob[:, :, :]), c1[:, :], ALU.add).then_inc(c_done.sem, 1)

            for buf in (*vM, *cv):
                nc.vector.memset(buf[:], 0.0).then_inc(v_zero.sem, 1)
            nc.vector.memset(act[:, FF:FFP], 0.0).then_inc(v_zero.sem, 1)
            dve.wait_ge(v_zero.sem, 5)
            dve.wait_ge(const_in.sem, 16)

            rounds(dve, named(a_mean_, a_normed_, a_tlo_, a_phi_q_, a_phi_k_, a_sput_, a_kq_, a_dinv_, a_y_, a_ylo_,
                              a_done_, b_mean_, b_normed_, b_pnorm_, b_diff_, b_ratio_, b_dlo_, b_rlo_, b_sbias_,
                              b_attn_, b_alo_, b_fdlo_, b_fput_, b_fmean_, b_fnormed_, b_haff_, b_hlo_, b_o_,
                              b_omean_, b_onormed_, b_done_, c_mean_, c_normed_, c_rscore_, c_before_,
                              c_selt_, c_hput_, c_hlo_, c_dinv_, c_o_, c_olo_, c_h2s_, c_h2put_, c_h2lo_,
                              c_y_, c_ylo_, c_done_)
                   | {f"a_kphi_{t}": k_phi(t) for t in range(TT)} | {f"a_scput_{g}": a_scput_(g) for g in range(8)}
                   | {f"b_glo_{j}": gelu_lo(j) for j in range(4)} | {f"c_smask_{g}": c_smask_(g) for g in range(4)}
                   | {f"c_gate_{j}": c_gate_(j) for j in range(2)} | {f"c_gtlo_{j}": c_gtlo_(j) for j in range(2)},
                   split_weights)

        @block.tensor
        def _(pe):
            mm = nc.tensor.matmul
            PASSES = ((0, 0), (0, 1), (1, 0))

            def split_product(out_, lhs, rhs, n):
                for a, (p, q) in enumerate(PASSES):
                    for k in range(n):
                        last = mm(out_, lhs(p, k), rhs(q, k), start=a == 0 and k == 0, stop=a == 2 and k == n - 1)
                return last

            def transposes(bank_, src, n_out, n_in):
                for o in range(n_out):
                    for i in range(n_in):
                        at = (o * n_in + i) * P
                        last = nc.tensor.transpose(bank_[:, at:at + P], src[:, i, o * P:(o + 1) * P], ident)
                return last

            def weights(b, n):
                if first(b):
                    pe.wait_ge(raw_lo.sem, n)

            def a_tp_(b):
                if not first(b):
                    pe.wait_ge(*a_y(b - 1))
                pe.wait_ge(*a_normed(b))
                transposes(a0, a_norm, DC, TT).then_inc(a_tp.sem, 1)

            def by_features(which, bk):
                for m in range(DC):
                    last = split_product(bk[:, m * T:(m + 1) * T],
                                         lambda p, k: wa[p][:, k, which * D + m * P:which * D + (m + 1) * P],
                                         lambda p, k: a_tr[p][:, k, :], DC)
                return last

            def a_q_(b):
                weights(b, LOADS_A)
                pe.wait_ge(*a_thi(b))
                pe.wait_ge(*a_tlo(b))
                if not first(b):
                    pe.wait_ge(*a_done(b - 1))
                by_features(0, a1).then_inc(a_qk.sem, 1)

            def a_k_(b):
                by_features(1, a2).then_inc(a_qk.sem, 1)

            def kv(t):
                def step(b):
                    weights(b, LOADS_A)
                    pe.wait_ge(*a_thi(b))
                    pe.wait_ge(*a_tlo(b))
                    if t == 1:
                        pe.wait_ge(*a_qout(b))
                    split_product((a0, a1)[t][:, :], lambda p, k: a_tr[p][:, k, t * P:(t + 1) * P],
                                  lambda p, k: wa[p][:, k, D:3 * D], DC).then_inc(a_kv.sem, 1)
                return step

            def a_ksum_(b):
                pe.wait_ge(*a_kphi(b))
                pe.wait_ge(*a_v(b, TT + 1))
                for c in range(DC):
                    cs = slice(c * P, (c + 1) * P)
                    mm(a0[:, c * T:(c + 1) * T], k_tok[:, 0, cs], C["tri_ones"], start=True, stop=False)
                    last = mm(a0[:, c * T + P:(c + 1) * T], k_tok[:, 1, cs], tri, start=False, stop=True)
                last.then_inc(a_ksum.sem, 1)

            def a_state_(b):
                pe.wait_ge(*a_kphi(b, 1))
                pe.wait_ge(*a_v(b, TT + 1))
                pe.wait_ge(*a_kout(b))
                for c in range(DC):
                    cs = slice(c * P, (c + 1) * P)
                    last = mm(a2[:, cs], k_tok[:, 0, cs], v0[:, cs], start=True, stop=True)
                last.then_inc(a_state.sem, 1)

            def a_den_(b):
                pe.wait_ge(*a_kq(b))
                for t in range(TT):
                    for c in range(DC):
                        last = mm(a0[:, t * NH + c * NH // DC:t * NH + (c + 1) * NH // DC],
                                  a_e0[:, c * T + t * P:c * T + (t + 1) * P], C["chunk_heads"], start=True, stop=True)
                last.then_inc(a_den.sem, 1)

            def a_rtp_(b):
                pe.wait_ge(*a_rden(b))
                transposes(a0, a_e1[:, :].rearrange("p (t d) -> p t d", t=TT), DC, TT).then_inc(a_rtp.sem, 1)

            GROUP = ((0, 0), (0, 1), (1, 0), (1, 1))

            def a_score_(g):
                def step(b):
                    t, bk, r = g // 4, (a1, a2)[g % 2], 32 * (g % 4)
                    if g == 0:
                        pe.wait_ge(*a_mask(b))
                        pe.wait_ge(*a_phi(b))
                        pe.wait_ge(*a_v(b))
                    if g == 1:
                        pe.wait_ge(*a_sput(b))
                    if g >= 2:
                        pe.wait_ge(*a_scput(b, g - 1))
                    for c in range(DC):
                        last = mm(bk[:, 2 * c * P:2 * (c + 1) * P], kT[r:r + 32, c, t * P:(t + 1) * P],
                                  qM[r:r + 32, c, t, :, :].rearrange("p m q -> p (m q)"), start=True, stop=True)
                    last.then_inc(a_score.sem, 1)
                return step

            def a_att_(g):
                def step(b):
                    t, r = g // 4, 32 * (g % 4)
                    if g == 0:
                        pe.wait_ge(*a_dput(b))
                    pe.wait_ge(*a_scput(b, g + 1))
                    if g == 4:
                        for c in range(DC):
                            mm(a0[:, c * T + P:(c + 1) * T], state[:, c * P:(c + 1) * P], qT[:, c, P:2 * P],
                               start=c == 0, stop=False, skip_group_check=True)
                    for j, (c, m) in enumerate(GROUP):
                        last = mm(a0[r:r + 32, c * T + t * P:c * T + (t + 1) * P],
                                  vM[m][:, t, c * P + r:c * P + r + 32],
                                  (a_s1, a_e0)[g % 2][:, j * P:(j + 1) * P], start=t == 0 and m == 0,
                                  stop=m == 1, skip_group_check=True)
                    last.then_inc(a_att.sem, 1)
                return step

            def a_proj_(b):
                pe.wait_ge(*a_yhi(b))
                pe.wait_ge(*a_ylo(b))
                for t in range(TT):
                    last = split_product(a1[:, t * D:(t + 1) * D], lambda p, k: a_tr[p][:, k, t * P:(t + 1) * P],
                                         lambda p, k: wp[p][:, k, :], DC)
                last.then_inc(a_proj.sem, 1)

            def b_dtp_(b):
                pe.wait_ge(*b_diff(b))
                transposes(b0, b_f0, DC, TT).then_inc(b_pairtp.sem, 1)

            def b_rtp_(b):
                pe.wait_ge(*b_ratio(b))
                if not first(b):
                    pe.wait_ge(*b_o(b - 1))
                transposes(b1, b_f1, DC, TT).then_inc(b_pairtp.sem, 1)

            def b_sid_(b):
                for s in (b_pairhi, b_pairlo):
                    pe.wait_ge(*s(b))
                for t in range(TT):
                    last = split_product(b0[:, t * T:(t + 1) * T],
                                         lambda p, k: b_s0[p][:, k * T + t * P:k * T + (t + 1) * P],
                                         lambda p, k: b_s1[p][:, k * T:(k + 1) * T], DC)
                last.then_inc(b_sid.sem, 1)

            def b_atp_(b):
                pe.wait_ge(*b_attn(b))
                transposes(b1, prob[:, TT:2 * TT, :], TT, TT).then_inc(b_atp.sem, 1)

            def b_fd_(b):
                for s in (b_ahi, b_alo, b_chi, b_clo):
                    pe.wait_ge(*s(b))
                for c in range(DC):
                    last = split_product(b0[:, c * T:(c + 1) * T],
                                         lambda p, k: b_s2[p][:, k * D + c * P:k * D + (c + 1) * P],
                                         lambda p, k: b_s0[p][:, k * T:(k + 1) * T], TT)
                last.then_inc(b_fd.sem, 1)

            def b_f_(b):
                weights(b, LOADS_A + LOADS_B)
                pe.wait_ge(*b_fdhi(b))
                pe.wait_ge(*b_fdlo(b))
                for t in range(TT):
                    last = split_product(b1[:, t * D:(t + 1) * D],
                                         lambda p, k: b_s1[p][:, k * T + t * P:k * T + (t + 1) * P],
                                         lambda p, k: wd[p][:, k, :], DC)
                last.then_inc(b_f.sem, 1)

            def b_htp_(b):
                pe.wait_ge(*b_fnormed(b))
                transposes(b0, prob, DC, TT).then_inc(b_htp.sem, 1)

            def mlp_up(j):
                def step(b):
                    if j == 0:
                        pe.wait_ge(*b_hhi(b))
                        pe.wait_ge(*b_hlo(b))
                    else:
                        pe.wait_ge(*b_gelu(b, 2 * j))
                    for n in range(2):
                        f = 2 * j + n
                        last = split_product(b0[:, n * T:(n + 1) * T], lambda p, k: w1[p][:, k, f * P:(f + 1) * P],
                                             lambda p, k: b_s0[p][:, k * T:(k + 1) * T], DC)
                    last.then_inc(b_up.sem, 1)
                return step

            def mlp_down(j):
                def step(b):
                    part = (b_s2, b_s1)[j % 2]
                    if j == 0:
                        pe.wait_ge(*b_fput(b))
                    pe.wait_ge(*b_ghi(b, j + 1))
                    pe.wait_ge(*b_glo(b, j + 1))
                    for t in range(TT):
                        for a, (p, q) in enumerate(PASSES):
                            for n in range(2):
                                last = mm(b1[:, t * D:(t + 1) * D], part[p][:, n * T + t * P:n * T + (t + 1) * P],
                                          w2[q][:, 2 * j + n, :], start=j == 0 and t == 0 and a == 0 and n == 0,
                                          stop=j == 3 and a == 2 and n == 1, skip_group_check=True)
                    last.then_inc(b_down.sem, 1)
                return step

            def c_sbc_(b):
                pe.wait_ge(*c_rscore(b))
                if not first(b):
                    pe.wait_ge(*c_y(b - 1))
                for t in range(TT):
                    last = nc.tensor.transpose(c0[:, t * P:(t + 1) * P], c_sc[:, t:t + 1].broadcast_to([P, P]), ident)
                last.then_inc(c_sbc.sem, 1)

            def c_rank_(b):
                pe.wait_ge(*c_before(b))
                if not first(b):
                    pe.wait_ge(*c_done(b - 1))
                for t in range(TT):
                    last = mm(c1[:, 0:T], ones_bf[:, :], before[:, t, :], start=t == 0, stop=t == TT - 1)
                last.then_inc(c_rank.sem, 1)

            def c_seltp_(b):
                pe.wait_ge(*c_selt(b))
                for t in range(TT):
                    last = nc.tensor.transpose(c2[:, t * R:(t + 1) * R], sel_t[:, t * P:(t + 1) * P].bitcast(F32),
                                               ident)
                last.then_inc(c_seltp.sem, 1)

            def c_xs_(b):
                for s in (c_sel, c_nhi, c_nlo):
                    pe.wait_ge(*s(b))
                for p in range(2):
                    for t in range(TT):
                        last = mm(c1[:, 0:D], sel[:, t, :], flat(act_t[p][:, 2 * t:2 * t + 2, :]),
                                  start=p == 0 and t == 0, stop=p == 1 and t == TT - 1)
                last.then_inc(c_xs.sem, 1)

            def c_htp_(b):
                pe.wait_ge(*c_h(b))
                for c in range(DC):
                    last = nc.tensor.transpose(c0[:, c * R:(c + 1) * R], c_h2[:, c * P:(c + 1) * P], ident)
                last.then_inc(c_htp.sem, 1)

            def c_qk_(b):
                if first(b):
                    pe.wait_ge(qk_in.sem, 16)
                pe.wait_ge(*c_hput(b))
                for m in range(2 * DC):
                    for k in range(DC):
                        last = mm(c2[:, m * R:(m + 1) * R], wcqk[:, k, m * P:(m + 1) * P], c_hT[:, k, :],
                                  start=k == 0, stop=k == DC - 1)
                last.then_inc(c_qk.sem, 1)

            def c_v_(b):
                weights(b, len(loads))
                pe.wait_ge(*c_hhi(b))
                pe.wait_ge(*c_hlo(b))
                split_product(c0[:, 0:D], lambda p, k: c_hs[p][:, k, :], lambda p, k: wcv[p][:, k, :], DC) \
                    .then_inc(c_v.sem, 1)

            def c_score_(g):
                def step(b):
                    r = 32 * g
                    if g == 0:
                        pe.wait_ge(*c_qkput(b))
                        pe.wait_ge(*c_xput(b))
                    if g >= 2:
                        pe.wait_ge(*c_etput(b, g - 1))
                    for c in range(DC):
                        last = mm((c1, c2)[g % 2][:, 2 * c * R:2 * (c + 1) * R], cq[r:r + 32, c, :],
                                  ck[r:r + 32, c, :, :].rearrange("p m k -> p (m k)"), start=True, stop=True)
                    last.then_inc(c_score.sem, 1)
                return step

            def c_etp_(g):
                def step(b):
                    pe.wait_ge(*c_exp(b, 4 * g + 4))
                    for j in range(4):
                        last = nc.tensor.transpose((c1, c2)[g % 2][:, j * R:(j + 1) * R],
                                                   flat(logits(g)[:, :, :])[:, j * R:(j + 1) * R], ident)
                    last.then_inc(c_etp.sem, 1)
                return step

            def c_att_(g):
                def step(b):
                    r = 32 * g
                    if g == 0:
                        pe.wait_ge(*c_vput(b))
                    pe.wait_ge(*c_etput(b, g + 1))
                    for j, (c, m) in enumerate(GROUP):
                        last = mm(c0[r:r + 32, c * R:(c + 1) * R], cv[m][:, c * P + r:c * P + r + 32],
                                  c_et[g % 2][:, j * R:(j + 1) * R], start=m == 0, stop=m == 1,
                                  skip_group_check=True)
                    last.then_inc(c_att.sem, 1)
                return step

            def c_dtp_(b):
                pe.wait_ge(*c_dinv(b))
                pe.wait_ge(*c_vput(b))
                for c in range(DC):
                    last = nc.tensor.transpose(c0[:, D + c * R:D + (c + 1) * R], c_rden[:, c * P:(c + 1) * P], ident)
                last.then_inc(c_dtp.sem, 1)

            def c_xo_(b):
                pe.wait_ge(*c_ohi(b))
                pe.wait_ge(*c_olo(b))
                split_product(c0[:, 0:D], lambda p, k: c_hs[p][:, k, :], lambda p, k: wo[p][:, k, :], DC) \
                    .then_inc(c_xo.sem, 1)

            def c_h2tp_(b):
                pe.wait_ge(*c_h2n_s(b))
                for c in range(DC):
                    last = nc.tensor.transpose(c1[:, c * R:(c + 1) * R], c_h2n[:, c * P:(c + 1) * P], ident)
                last.then_inc(c_h2tp.sem, 1)

            def c_gu_(j):
                def step(b):
                    n = (FG, FF - FG)[j]
                    if j:
                        pe.wait_ge(*c_gate(b, 2))
                    else:
                        pe.wait_ge(*c_h2hi(b))
                        pe.wait_ge(*c_h2lo(b))
                    for which, bk in enumerate((c1, c2)):
                        last = split_product(bk[:, 0:n], lambda p, k: c_hs[p][:, k, :],
                                             lambda p, k: wgu[p][:, k, which * FF + j * FG:which * FF + j * FG + n],
                                             DC)
                    last.then_inc(c_gu.sem, 1)
                return step

            def c_gtp_(j):
                def step(b):
                    bk, lo, hi = ((c1, 0, 4), (c2, 4, 6))[j]
                    pe.wait_ge(*c_gate(b))
                    for f in range(lo, hi):
                        last = nc.tensor.transpose(bk[:, (f - lo) * R:(f - lo + 1) * R], act[:, f * P:(f + 1) * P],
                                                   ident)
                    last.then_inc(c_gtp.sem, 1)
                return step

            def c_ff_(b):
                pe.wait_ge(*c_gthi(b))
                pe.wait_ge(*c_gtlo(b))
                split_product(c0[:, D:2 * D], lambda p, k: act_t[p][:, k, :], lambda p, k: w3[p][:, k, :], FFP // P) \
                    .then_inc(c_ff.sem, 1)

            def c_scat_(b):
                pe.wait_ge(*c_yhi(b))
                pe.wait_ge(*c_ylo(b))
                for t in range(TT):
                    for p in range(2):
                        last = mm(c1[:, t * D:(t + 1) * D], sel_t[:, t * P:(t + 1) * P], flat(c_hs[p][:, :, :]),
                                  start=p == 0, stop=p == 1)
                last.then_inc(c_scat.sem, 1)

            pe.wait_ge(const_in.sem, 16)
            pe.wait_ge(ones_set.sem, 1)
            pe.wait_ge(v_zero.sem, 5)

            rounds(pe, named(a_tp_, a_q_, a_k_, a_ksum_, a_state_, a_den_, a_rtp_, a_proj_, b_dtp_, b_rtp_, b_sid_, b_atp_, b_fd_,
                             b_f_, b_htp_, c_sbc_, c_rank_, c_seltp_, c_xs_, c_htp_, c_qk_, c_v_, c_dtp_, c_xo_,
                             c_h2tp_, c_ff_, c_scat_)
                   | {f"a_kv_{t}": kv(t) for t in range(TT)}
                   | {f"a_score_{g}": a_score_(g) for g in range(8)} | {f"a_att_{g}": a_att_(g) for g in range(8)}
                   | {f"b_up_{j}": mlp_up(j) for j in range(4)} | {f"b_down_{j}": mlp_down(j) for j in range(4)}
                   | {f"c_score_{g}": c_score_(g) for g in range(4)} | {f"c_etp_{g}": c_etp_(g) for g in range(4)}
                   | {f"c_att_{g}": c_att_(g) for g in range(4)} | {f"c_gu_{j}": c_gu_(j) for j in range(2)}
                   | {f"c_gtp_{j}": c_gtp_(j) for j in range(2)})


def constants():
    p = np.arange(P)
    t = np.arange(T)
    c = np.zeros((P, NCONST), np.float32)
    c[:, CONST["ident2"]] = np.stack([t[None] == n * P + p[:, None] for n in range(TT)], 1).reshape(P, -1)
    c[:, CONST["tri_ones"]] = p[:, None] <= t[None]
    c[:, CONST["neg_mask"]] = np.where(p[None] > p[:, None], NEG, 0.0)
    c[:, CONST["head_block"]] = p[:, None] // HD == p[None] // HD
    c[:, CONST["tie_mask"]] = np.stack([n * P + p[:, None] < t[None] for n in range(TT)], 1).reshape(P, -1)
    c[:, CONST["iota"]] = p[:, None]
    even = (p // HD % 2 == 0).astype(np.float32)[:, None]
    c[:, CONST["even"]], c[:, CONST["odd"]] = even, 1 - even
    c[:, CONST["minus_half"]] = -0.5
    c[:, CONST["prob_bias"]] = 0.5
    c[:, CONST["chunk_heads"]] = p[:, None] // HD == np.arange(NH // DC)[None]
    return c


def kernel(**inputs):
    import concourse.bacc as bacc
    from concourse.bass_utils import run_bass_kernel_spmd

    a = {k: np.asarray(v) for k, v in inputs.items()}

    def by_input(w, n_in):
        return np.ascontiguousarray(w.T.reshape(n_in, P, w.shape[0]).transpose(1, 0, 2))

    def column(v):
        return v.reshape(-1, P).T

    w3 = np.zeros((D, FFP), np.float32)
    w3[:, :FF] = a["L0_ffn_W3"]
    gu = np.concatenate([a["L0_ffn_W1"], a["L0_ffn_W2"]], 0)
    by_row = [a[f"L0_{n}"] for n in ("xattn_ln_g", "xattn_ln_b", "xattn_b2", "xattn_b_diff", "ffn_w_router")]
    by_col = [a[f"L0_{n}"] for n in ("xattn_ln_g", "xattn_ln_b", "ffn_g1", "ffn_g2", "xattn_b1")]
    arrays = {
        "x": a["x"].reshape(B * T, D),
        "ctx": a["ctx_1024"].reshape(B * T, D),
        "consts": constants(),
        "vec_bc": np.ascontiguousarray(np.broadcast_to(np.stack(by_row)[None], (P, 5, D))),
        "vec_cols": np.ascontiguousarray(np.concatenate([column(v) for v in by_col], 1)),
        "w_a": by_input(a["L0_attn_w_attn"], DC),
        "w_proj": by_input(a["L0_attn_w_proj"], DC).reshape(P, -1),
        "w_diff": by_input(a["L0_xattn_W_diff"], DC).reshape(P, -1),
        "w_1": by_input(a["L0_xattn_W1"], DC),
        "w_2": by_input(a["L0_xattn_W2"], MLP // P),
        "w_cqk": by_input(a["L0_ffn_W_qkv"][:2 * D], DC),
        "w_cv": by_input(a["L0_ffn_W_qkv"][2 * D:], DC).reshape(P, -1),
        "w_out": by_input(a["L0_ffn_W_out"], DC).reshape(P, -1),
        "w_gu": by_input(gu, DC),
        "w_3": by_input(w3, FFP // P),
    }
    nc = bacc.Bacc("TRN2", target_bir_lowering=False, num_devices=1)
    args = [nc.dram_tensor(f"in_{k}", v.shape, F32, kind="ExternalInput").ap() for k, v in arrays.items()]
    out = nc.dram_tensor("out_0", (B * T, D), F32, kind="ExternalOutput").ap()
    decoder(nc, *args, out)
    r = run_bass_kernel_spmd(nc, [{f"in_{k}": v for k, v in arrays.items()}], core_ids=[0])
    return r.results[0]["out_0"].reshape(B, T, D)
```
